# Optimizing a Trainium2 kernel written in Bass

```python
import numpy as np
import jax
import jax.numpy as jnp

def _softmax(x, axis=-1):
    return jax.nn.softmax(x, axis=axis)

def _gelu(x):
    return jax.nn.gelu(x, approximate=True)

def _silu(x):
    return jax.nn.silu(x)

def _sigmoid(x):
    return jax.nn.sigmoid(x)

def _layernorm(x, axis=-1, eps=1e-05):
    m = jnp.mean(x, axis=axis, keepdims=True)
    v = jnp.var(x, axis=axis, keepdims=True)
    return (x - m) / jnp.sqrt(v + eps)

def _scatter_add(tgt, idx, src, axis=0):
    return tgt.at[idx].add(src)

def _segment_sum(src, seg, n):
    return jax.ops.segment_sum(src, seg, n)
kernel_name = 'mk_cond_resid_d1_seqx_r4_c2baba'

def setup_inputs(seed: int=0):
    np.random.seed(seed)
    _w = jnp.asarray

    def _rec_inputs():
        import jax
        import jax.numpy as jnp
        _rk = jax.random.key(seed)
        x = 7.22e-05 + 1 * jax.random.normal(jax.random.fold_in(_rk, 1), (2, 1024, 256), jnp.float32)
        _lenS = 1024 - jax.random.randint(jax.random.fold_in(_rk, 7), (2,), 0, max(1, 1024 // 4) + 1, jnp.int32)
        _lenS2 = 1024 - jax.random.randint(jax.random.fold_in(_rk, 8), (2,), 0, max(1, 1024 // 4) + 1, jnp.int32)
        cond_2048 = 0.997298 + 0.498944 * jax.random.normal(jax.random.fold_in(_rk, 11), (2, 512), jnp.float32)
        return (x, cond_2048)
    x, cond_2048 = _rec_inputs()

    def _L0_cond_setup():
        import jax, jax.numpy as jnp
        import numpy as np
        EPS_IN = 1e-05
        EPS_DM = 1e-08

        def _dcoef(weight, style):
            return jax.lax.rsqrt(jnp.einsum('oi,bi->bo', jnp.square(weight), jnp.square(style)) + EPS_DM)
        key = jax.random.key(seed)
        ks = jax.random.split(key, 7)
        B, S, H = (8, 256, 256)
        lim = 1.0 / np.sqrt(H)
        u = lambda k, shp: jax.random.uniform(k, shp, jnp.float32, -lim, lim)
        return {'x': jax.random.normal(ks[0], (B, S, H), jnp.float32), 'q_weight': u(ks[1], (H, H)), 'k_weight': u(ks[2], (H, H)), 'v_weight': u(ks[3], (H, H)), 'w_weight': u(ks[4], (H, H)), 'u_weight': u(ks[5], (H, H)), 'styles': jax.random.normal(ks[6], (B, 2 * H), jnp.float32) * 0.5 + 1.0, 'num_heads': 16}
    _L0_cond_all = _L0_cond_setup()
    _L0_cond_in = {k: v for k, v in _L0_cond_all.items() if k in ('q_weight', 'k_weight', 'v_weight', 'w_weight', 'u_weight')}
    del _L0_cond_all
    return {'x': x, 'cond_2048': cond_2048, 'L0_cond_q_weight': _L0_cond_in['q_weight'], 'L0_cond_k_weight': _L0_cond_in['k_weight'], 'L0_cond_v_weight': _L0_cond_in['v_weight'], 'L0_cond_w_weight': _L0_cond_in['w_weight'], 'L0_cond_u_weight': _L0_cond_in['u_weight']}

def reference(x, cond_2048, L0_cond_q_weight, L0_cond_k_weight, L0_cond_v_weight, L0_cond_w_weight, L0_cond_u_weight):
    import jax
    import jax.numpy as jnp

    def _L0_cond_ref(x, q_weight, k_weight, v_weight, w_weight, u_weight, styles, num_heads):
        import jax, jax.numpy as jnp
        import numpy as np
        EPS_IN = 1e-05
        EPS_DM = 1e-08

        def _dcoef(weight, style):
            return jax.lax.rsqrt(jnp.einsum('oi,bi->bo', jnp.square(weight), jnp.square(style)) + EPS_DM)
        B, S, H = x.shape
        nh = num_heads
        d = H // nh
        scale = jnp.asarray(d, x.dtype) ** (-0.5)
        s1 = styles[:, :H]
        s2 = styles[:, H:]
        x = x * s1[:, None, :]
        mu = jnp.mean(x, axis=-1, keepdims=True)
        var = jnp.mean(jnp.square(x - mu), axis=-1, keepdims=True)
        x = (x - mu) * jax.lax.rsqrt(var + EPS_IN)
        q_dc = _dcoef(q_weight, s1)
        k_dc = _dcoef(k_weight, s1)
        v_dc = _dcoef(v_weight, s1)
        w_dc = _dcoef(w_weight, s2)
        u_dc = _dcoef(u_weight, s2)

        def heads(t):
            return t.reshape(B, S, nh, d).transpose(0, 2, 1, 3)
        q = heads(jnp.einsum('bsh,oh->bso', x, q_weight) * q_dc[:, None, :])
        k = heads(jnp.einsum('bsh,oh->bso', x, k_weight) * k_dc[:, None, :])
        v_flat = jnp.einsum('bsh,oh->bso', x, v_weight) * v_dc[:, None, :] * s2[:, None, :]
        skip = v_flat
        v = heads(v_flat)
        attn = jnp.einsum('bhqd,bhkd->bhqk', q, k) * scale
        attn = jax.nn.softmax(attn, axis=-1)
        out = jnp.einsum('bhqk,bhkd->bhqd', attn, v).transpose(0, 2, 1, 3).reshape(B, S, H)
        out = jnp.einsum('bsh,oh->bso', out, w_weight) * w_dc[:, None, :]
        skip = jnp.einsum('bsh,oh->bso', skip, u_weight) * u_dc[:, None, :]
        return out + skip
    x = x + _L0_cond_ref(x, L0_cond_q_weight, L0_cond_k_weight, L0_cond_v_weight, L0_cond_w_weight, L0_cond_u_weight, cond_2048, 16)
    return x

_drawn_inputs = setup_inputs


def setup_inputs(seed=0):
    import zlib

    import numpy as np

    out = dict(_drawn_inputs(seed))
    spreads = {}
    factors = {}
    for name, (base, spread) in spreads.items():
        noise = np.random.default_rng([zlib.crc32(name.encode()), seed]).standard_normal(out[name].shape)
        drawn = base * np.exp(spread * noise) if base else spread * noise
        out[name] = jnp.asarray(drawn.astype(out[name].dtype))
    for name, factor in factors.items():
        out[name] = (out[name] * factor).astype(out[name].dtype)
    return out
```

```python
from contextlib import ExitStack

import concourse.bass as bass
from concourse import mybir

F32 = mybir.dt.float32
BF16 = mybir.dt.bfloat16
ALU = mybir.AluOpType
ACT = mybir.ActivationFunctionType
AX = mybir.AxisListType

P = 128
NH = 16
Q, K, V, W, U = range(5)
Q_PIECES = (0, 1, 2, 0, 1, 0)
K_PIECES = (0, 0, 0, 1, 1, 2)


def cond_attention(nc: bass.Bass, x, cond, wq, wk, wv, ww, wu, out):
    B, S, H = x.shape
    D = H // NH
    HH = H // P
    TB = S // P
    NT = B * TB
    G = B * HH
    HG = NH // HH
    PG = HG // 2
    PAIRS = G * PG
    HEADS = 2 * PAIRS
    C = S // 512
    KR = len(Q_PIECES) * D
    ROWS = KR + 3
    VW = 2 * D
    STEPS = TB
    CH = TB * C
    EARLY = 3
    SCALE = float(D) ** -0.5

    x_v = x.rearrange("b (t p) h -> p (b t) h", p=P)
    out_v = out.rearrange("b (t p) h -> p (b t) h", p=P)
    w_in = (wq, wk, wv, ww, wu)
    piece_dram = [nc.dram_tensor(n, (G, HG, 3, D, S), BF16, kind="Internal").ap()
                  for n in ("q_pieces", "k_pieces")]
    den_dram = nc.dram_tensor("denominators", (HEADS, S), F32, kind="Internal").ap()
    rec_dram = nc.dram_tensor("reciprocals", (HEADS, S), F32, kind="Internal").ap()

    with ExitStack() as ctx:
        def sb(name, shape, dt):
            return ctx.enter_context(nc.sbuf_tensor(name, shape, dt))

        def sem(name):
            return ctx.enter_context(nc.semaphore(name))

        ps = ctx.enter_context(nc.psum_tensor("ps", [P, 8, 512], F32))
        MAX_BANKS, ST_BANK, PV_BANK = 3, 3, 7
        JOB_BANKS = 5

        X = sb("X", [P, NT, H], F32)
        xs = sb("xs", [P, NT, H], F32)
        xT = sb("xT", [P, HH, B * S], F32)
        Vall = sb("Vall", [P, G, TB, P], F32)
        prob = sb("prob", [P, 4, 2, S], F32)
        qst = sb("qst", [P, 4, 2, S], BF16)
        kst = sb("kst", [P, 4, 2, S], BF16)
        vbuf = sb("vbuf", [P, PG, TB, 2, VW], F32)
        ob = sb("ob", [P, 2, 512], F32)
        Wr = sb("Wr", [P, 5, HH, H], F32)
        Wsc = sb("Wsc", [P, 2, HH, H], F32)
        WT = sb("WT", [P, 3, HH, H], F32)
        WUT = sb("WUT", [P, 2, B, HH, H], F32)
        Mb = sb("Mb", [P, B, HH, H], F32)
        shared = sb("shared", [P, 7 * S], F32)
        AT = shared[:, 0:G * S].rearrange("p (g t) -> p g t", g=G)
        RD = shared[:, G * S:(G + 3) * S].rearrange("p (g t) -> p g t", g=3)
        full = shared[:, 0:2 * S].rearrange("p (i t) -> p i t", i=2)
        rest = shared[:, 2 * S:4 * S].rearrange("p (i t) -> p i t", i=2)
        pieces = shared[:, 4 * S:7 * S].bitcast(BF16).rearrange("p (i c t) -> p i c t", i=2, c=3)
        wsty = shared[:, 3 * S:3 * S + 2 * HH * H].rearrange("p (i a h) -> p i a h", i=2, a=HH)
        cb = sb("cb", [P, B, 2, H], F32)
        s2col = sb("s2col", [P, B, HH], F32)
        dsum = sb("dsum", [P, 5, B, HH], F32)
        dcoef = sb("dcoef", [P, 5, B, HH], F32)
        vs2 = sb("vs2", [P, B, HH], F32)
        stats = sb("stats", [P, NT, 6], F32)
        mv = sb("mv", [P, NT, 2], F32)
        vareps = sb("vareps", [P, NT], F32)
        rstd = sb("rstd", [P, NT], F32)
        minus_half = sb("minus_half", [P, 5 * G], F32)
        identf = sb("identf", [P, P], F32)
        identb = sb("identb", [P, P], BF16)
        mx = sb("mx", [P, 2, TB, C], F32)
        nm = sb("nm", [P, 2, TB], F32)
        nmr = sb("nmr", [P, 2, 2, TB], F32)
        mpc = sb("mpc", [P, 2, 3, TB], BF16)
        mT = sb("mT", [3 * TB, 4, P], BF16)
        junk = shared[:, 2 * S:2 * S + H]
        den = xs[:, 4, 0:(G - 1) * S * HG // P]
        denl = xs[:, 5, 0:S * HG // P]
        yb = xs[:, 0:4]

        warm = sb("warm", [P, 1], F32)
        zeros = sb("zeros", [P, TB], F32)

        x_loaded = [sem(f"x_loaded{b}") for b in range(B)]
        w_loaded = [sem(f"w_loaded{w}") for w in range(5)]
        cond_loaded, s2_loaded = sem("cond_loaded"), sem("s2_loaded")
        ident_ready, consts_ready, pool_own = sem("ident_ready"), sem("consts_ready"), sem("pool_own")
        styled, squared = sem("styled"), sem("squared")
        dcoef_ready, vs2_ready = sem("dcoef_ready"), sem("vs2_ready")
        dve_own, var_ready, rstd_ready, xhat_ready = sem("dve_own"), sem("var_ready"), sem("rstd_ready"), sem("xhat_ready")
        w_scaled = sem("w_scaled")
        job_done, job_act, job_dve = sem("job_done"), sem("job_act"), sem("job_dve")
        split_rest, split_last = sem("split_rest"), sem("split_last")
        stored = [sem(f"stored{i}") for i in range(2)]
        stack_loaded = [sem(f"stack_loaded{i}") for i in range(4)]
        chunk_done, max_done, negmax_ready = sem("chunk_done"), sem("max_done"), sem("negmax_ready")
        negmax_split, msplit_own = sem("negmax_split"), sem("msplit_own")
        turned, mrow_copied = sem("turned"), sem("mrow_copied")
        mrow_loaded = [sem(f"mrow_loaded{i}") for i in range(4)]
        st_done, exp_done, pv_done = sem("st_done"), sem("exp_done"), sem("pv_done")
        v_ready, pv_free = sem("v_ready"), sem("pv_free")
        ob_moved = [sem(f"ob_moved{i}") for i in range(2)]
        ones_ready = sem("ones_ready")
        den_loaded, rec_ready, rec_stored, rd_loaded, at_ready = (
            sem("den_loaded"), sem("rec_ready"), sem("rec_stored"), sem("rd_loaded"), sem("at_ready"))
        y_done, y_added = sem("y_done"), sem("y_added")
        y_stored = [sem(f"y_stored{i}") for i in range(4)]

        jobs = [("wt", w) for w in (Q, K, V)]
        jobs += [("xt", t) for t in range(TB // 2)]
        jobs += [("qk", 0, m, c) for m in (Q, K) for c in range(C)]
        jobs += [("xt", t) for t in range(TB // 2, TB)]
        jobs += [("qk", 1, m, c) for m in (Q, K) for c in range(C)]
        jobs += [("v", t) for t in range(TB // 2)]
        jobs += [("qk", g, m, c) for g in (2, 3) for m in (Q, K) for c in range(C)]
        jobs += [("v", t) for t in range(TB // 2, TB)]
        jobs += [("wu", i, b) for b in range(B) for i in range(2)]
        jobs += [("m", b) for b in range(B)]
        on_dve = [j[0] in ("wu", "m") for j in jobs]
        FIRST_CHUNK = 15

        def chunks_after(n):
            last = len(jobs) - 1
            if n < FIRST_CHUNK:
                return []
            at = 2 * (n - FIRST_CHUNK)
            upto = EARLY * CH + 4 if n == last else min(at + 2, EARLY * CH + 4)
            return [divmod(i, CH) for i in range(at, upto)]

        def emptied(eng, n):
            count = sum(d == on_dve[n] for d in on_dve[:n + 1])
            eng.wait_ge(job_dve if on_dve[n] else job_act, count)

        def qk_index(g, m):
            return 2 * g + m

        block = ctx.enter_context(nc.Block())

        @block.sync
        def _(sp):
            sp.dma_start(cb[:, 0], cond[0].rearrange("(s h) -> s h", s=2).partition_broadcast(P)).then_inc(cond_loaded, 16)
            sp.dma_start(cb[:, 1], cond[1].rearrange("(s h) -> s h", s=2).partition_broadcast(P)).then_inc(cond_loaded, 16)
            sp.dma_start(X[:, 0:TB], x_v[:, 0:TB]).then_inc(x_loaded[0], 16)
            for w in (V, W, U):
                sp.dma_start(Wr[:, w], w_in[w].rearrange("(a p) h -> p a h", p=P)).then_inc(w_loaded[w], 16)
            for b in range(B):
                with nc.allow_non_contiguous_dma(reason="one style for each partition"):
                    sp.dma_start(s2col[:, b], cond[b, H:2 * H].rearrange("(a p) -> p a", p=P)).then_inc(s2_loaded, 16)
            sp.dma_start(X[:, TB:NT], x_v[:, TB:NT]).then_inc(x_loaded[1], 16)

            def store_pieces(g, m):
                i = qk_index(g, m)
                sp.wait_ge(split_last, i + 1)
                for c in range(3):
                    sp.dma_start(piece_dram[m][g, :, c], pieces[:, i % 2, c]).then_inc(stored[i % 2], 16)

            def load_stacks(g, j):
                for m, stack in ((Q, qst), (K, kst)):
                    src = piece_dram[m][g, 2 * j:2 * j + 2].rearrange("h c d t -> (c d) h t")
                    if m == Q:
                        runs = ((0, 0, 3), (3, 0, 2), (5, 0, 1))
                    else:
                        runs = tuple((r, K_PIECES[r], 1) for r in range(6))
                    for row, piece, n in runs:
                        sp.dma_start(stack[row * D:(row + n) * D, j], src[piece * D:(piece + n) * D]).then_inc(stack_loaded[j], 16)

            def move_mrow(h, hg):
                sp.wait_ge(mrow_copied, h + 1)
                for c in range(3):
                    sp.dma_start(qst[KR + c:KR + c + 1, hg // 2, hg % 2].rearrange("o (a t) -> o a t", a=TB),
                                 mT[c * TB:(c + 1) * TB, hg % 4]).then_inc(mrow_loaded[hg // 2], 16)

            def move_output(g, j):
                sp.wait_ge(pv_free, g * PG + j + 2)
                for hd in range(2):
                    for c in range(C):
                        row = 32 * (2 * hd + c)
                        sp.dma_start(AT[(2 * j + hd) * D:(2 * j + hd + 1) * D, g, c * 512:(c + 1) * 512],
                                     ob[row:row + D, j % 2]).then_inc(ob_moved[j % 2], 16)
                sp.dma_start(den_dram[bass.ds(g * HG + 2 * j, 2)].rearrange("h (c t) -> (h c) t", c=C),
                             ob[D:P:32, j % 2]).then_inc(ob_moved[j % 2], 16)

            for g in range(G):
                for m in (Q, K):
                    store_pieces(g, m)
                if g == 0:
                    sp.wait_ge(stored[0], 48)
                    sp.wait_ge(stored[1], 48)
                    load_stacks(0, 0)
                    load_stacks(0, 1)
            move_mrow(0, 0)
            move_mrow(1, 1)
            for i in range(2):
                sp.wait_ge(stored[i], 48 * G)

            def pair(g, j, final):
                p = g * PG + j
                if not final or j < 2:
                    sp.wait_ge(st_done, 2 * STEPS * p + 1)
                    load_stacks(g + (j + 2) // PG, (j + 2) % PG)
                if not final or j < 3:
                    move_mrow(2 * p + 2, (2 * j + 2) % HG)
                    move_mrow(2 * p + 3, (2 * j + 3) % HG)
                move_output(g, j)

            with sp.Fori(0, G - 1) as g:
                for j in range(PG):
                    pair(g, j, False)

            def reciprocals(g0, n, tile, k):
                rows = slice(g0 * HG, (g0 + n) * HG)
                flat = den_dram[rows].rearrange("h t -> (h t)").rearrange("(p f) -> p f", p=P)
                back = rec_dram[rows].rearrange("h t -> (h t)").rearrange("(p f) -> p f", p=P)
                sp.dma_start(tile, flat).then_inc(den_loaded, 16)
                sp.wait_ge(rec_ready, k + 1)
                sp.dma_start(back, tile).then_inc(rec_stored, 16)
                sp.wait_ge(rec_stored, 16 * (k + 1))
                for i in range(n):
                    g = g0 + i
                    for h in range(HG):
                        sp.dma_start(RD[h * D:(h + 1) * D, i],
                                     rec_dram[g * HG + h].partition_broadcast(D)).then_inc(rd_loaded, 16)

            for i in range(2):
                sp.wait_ge(ob_moved[i], 16 * 5 * 2 * (G - 1))
            pair(G - 1, 0, True)
            pair(G - 1, 1, True)
            reciprocals(0, G - 1, den, 0)
            pair(G - 1, 2, True)
            pair(G - 1, 3, True)
            for i in range(2):
                sp.wait_ge(ob_moved[i], 16 * 5 * 2 * G)
            sp.wait_ge(at_ready, G - 1)
            reciprocals(G - 1, 1, denl, 1)

        @block.gpsimd
        def _(pool):
            own = 0
            nc.gpsimd.memset(identf[:], 0.0).then_inc(pool_own, 1)
            nc.gpsimd.memset(zeros[:], 0.0)
            nc.gpsimd.memset(minus_half[:], -0.5).then_inc(pool_own, 1)
            pool.wait_ge(pool_own, 2)
            nc.gpsimd.affine_select(out=identf[:], in_=identf[:], compare_op=ALU.not_equal, fill=1.0, base=0,
                                    pattern=[[-1, P]], channel_multiplier=1).then_inc(pool_own, 1)
            pool.wait_ge(pool_own, 3)
            nc.gpsimd.tensor_copy(identb[:], identf[:]).then_inc(ident_ready, 1)
            pool.wait_ge(ident_ready, 1)
            nc.gpsimd.memset(kst[KR:ROWS], 1.0).then_inc(ones_ready, 1)
            pool.wait_ge(ones_ready, 1)
            nc.gpsimd.memset(vbuf[:], 1.0).then_inc(ones_ready, 1)

            def inverse_roots(b):
                t = slice(b * TB, (b + 1) * TB)
                pool.wait_ge(var_ready, b + 1)
                nc.gpsimd.tensor_scalar(vareps[:, t], mv[:, t, 1], 1e-5, None, ALU.add).then_inc(pool_own, 1)
                pool.wait_ge(pool_own, 4 + b)
                nc.gpsimd.tensor_tensor(rstd[:, t], vareps[:, t], minus_half[:, 0:TB], ALU.pow).then_inc(rstd_ready, 1)

            inverse_roots(0)
            flat = dsum[:].rearrange("p w b a -> p (w b a)")
            pool.wait_ge(squared, 5 * G)
            nc.gpsimd.tensor_scalar(flat, flat, 1e-8, None, ALU.add).then_inc(dcoef_ready, 1)
            pool.wait_ge(dcoef_ready, 1)
            nc.gpsimd.tensor_tensor(dcoef[:].rearrange("p w b a -> p (w b a)"), flat, minus_half[:], ALU.pow).then_inc(dcoef_ready, 1)
            pool.wait_ge(dcoef_ready, 2)
            pool.wait_ge(s2_loaded, 32)
            nc.gpsimd.tensor_tensor(vs2[:].rearrange("p b a -> p (b a)"), dcoef[:, V].rearrange("p b a -> p (b a)"),
                                    s2col[:].rearrange("p b a -> p (b a)"), ALU.mult).then_inc(vs2_ready, 1)

            def split_max(h, hb):
                pool.wait_ge(negmax_ready, h + 1)
                nc.gpsimd.tensor_tensor(mpc[:, hb, 0], nm[:, hb], zeros[:], ALU.add).then_inc(msplit_own, 1)
                pool.wait_ge(msplit_own, 4 * h + 1)
                nc.gpsimd.tensor_tensor(nmr[:, hb, 0], nm[:, hb], mpc[:, hb, 0], ALU.subtract).then_inc(msplit_own, 1)
                pool.wait_ge(msplit_own, 4 * h + 2)
                nc.gpsimd.tensor_tensor(mpc[:, hb, 1], nmr[:, hb, 0], zeros[:], ALU.add).then_inc(msplit_own, 1)
                pool.wait_ge(msplit_own, 4 * h + 3)
                nc.gpsimd.tensor_tensor(nmr[:, hb, 1], nmr[:, hb, 0], mpc[:, hb, 1], ALU.subtract).then_inc(msplit_own, 1)
                pool.wait_ge(msplit_own, 4 * h + 4)
                nc.gpsimd.tensor_tensor(mpc[:, hb, 2], nmr[:, hb, 1], zeros[:], ALU.add).then_inc(negmax_split, 1)

            def values(g, j):
                nc.gpsimd.tensor_copy(vbuf[:, j, :, :, 0:D],
                                      Vall[:, g, :, 2 * j * D:2 * (j + 1) * D].rearrange("p t (h d) -> p t h d", h=2)
                                      ).then_inc(v_ready, 1)

            for n, job in enumerate(jobs):
                if job[0] == "xt" and job[1] == TB // 2:
                    inverse_roots(1)
                if job[0] == "qk" and job[3] == C - 1:
                    i = qk_index(job[1], job[2])
                    pool.wait_ge(split_rest, 2 * (i + 1))
                    nc.gpsimd.tensor_tensor(pieces[:, i % 2, 2], rest[:, i % 2], pieces[:, i % 2, 1],
                                            ALU.subtract).then_inc(split_last, 1)
                if job == ("v", TB // 2 - 1):
                    emptied(pool, n)
                    pool.wait_ge(ones_ready, 2)
                    values(0, 0)
                for h, i in chunks_after(n):
                    if i == CH - 1:
                        split_max(h, h % 2)

            emptied(pool, jobs.index(("v", TB - 1)))

            with pool.Fori(0, G - 1) as g:
                for j in range(PG):
                    p = g * PG + j
                    split_max(2 * p + 3, 1)
                    values(g + (j + 1) // PG, (j + 1) % PG)
                    split_max(2 * p + 4, 0)
            for j in range(PG - 1):
                p = (G - 1) * PG + j
                if 2 * p + 3 < HEADS:
                    split_max(2 * p + 3, 1)
                values(G - 1, j + 1)
                if 2 * p + 4 < HEADS:
                    split_max(2 * p + 4, 0)

        @block.vector
        def _(dve):
            own = [0]

            def after(ins):
                own[0] += 1
                ins.then_inc(dve_own, 1)
                dve.wait_ge(dve_own, own[0])

            def norm_stats(b):
                t = slice(b * TB, (b + 1) * TB)
                dve.wait_ge(x_loaded[b], 16)
                after(nc.vector.tensor_tensor(xs[:, t], X[:, t], cb[:, b, 0:1].to_broadcast([P, TB, H]), ALU.mult))
                for i in range(b * TB, (b + 1) * TB):
                    last = nc.vector.bn_stats(stats[:, i], xs[:, i])
                after(last)
                for i in range(b * TB, (b + 1) * TB):
                    last = nc.vector.bn_aggr(mv[:, i], stats[:, i])
                last.then_inc(var_ready, 1)

            def norm_apply(b):
                dve.wait_ge(rstd_ready, b + 1)
                for i in range(b * TB, (b + 1) * TB):
                    nc.vector.tensor_scalar(xs[:, i], xs[:, i], mv[:, i, 0:1], rstd[:, i:i + 1],
                                            ALU.subtract, ALU.mult).then_inc(xhat_ready, 1)

            def style(n, w, b):
                dve.wait_ge(w_loaded[w], 16)
                if n >= 2:
                    dve.wait_ge(squared, HH * (n - 1))
                part = 0 if w in (Q, K, V) else 1
                nc.vector.tensor_tensor(wsty[:, n % 2], Wr[:, w], cb[:, b, part:part + 1].to_broadcast([P, HH, H]),
                                        ALU.mult).then_inc(styled, 1)

            dve.wait_ge(cond_loaded, 32)
            norm_stats(0)
            for n in range(4):
                style(n, n // B, n % B)
            norm_apply(0)
            for n in range(4, 5 * B):
                style(n, n // B, n % B)

            def reduce_chunk(h, i, hb):
                bank = (i if i < 6 else i + 1) % MAX_BANKS
                dve.wait_ge(chunk_done, h * CH + i + 1)
                nc.vector.tensor_reduce(mx[:, hb, i // C, i % C:i % C + 1], ps[:, bank], AX.X, ALU.max).then_inc(max_done, 1)
                if i == CH - 1:
                    dve.wait_ge(max_done, (h + 1) * CH)
                    nc.vector.tensor_reduce(nm[:, hb], mx[:, hb], AX.X, ALU.max, negate=True).then_inc(negmax_ready, 1)

            for n, job in enumerate(jobs):
                if job == ("xt", TB // 2):
                    norm_stats(1)
                    norm_apply(1)
                if job[0] == "qk" and job[3] == C - 1:
                    i = qk_index(job[1], job[2])
                    emptied(dve, n)
                    if i >= 2:
                        dve.wait_ge(split_last, i - 1)
                        dve.wait_ge(stored[i % 2], 48 * (i // 2))
                    nc.vector.tensor_tensor(rest[:, i % 2], full[:, i % 2], pieces[:, i % 2, 0],
                                            ALU.subtract).then_inc(split_rest, 1)
                    dve.wait_ge(split_rest, 2 * i + 1)
                    nc.vector.tensor_copy(pieces[:, i % 2, 1], rest[:, i % 2]).then_inc(split_rest, 1)
                if job[0] == "wu":
                    _, i, b = job
                    dve.wait_ge(job_done, n + 1)
                    dve.wait_ge(vs2_ready, 1)
                    bank = ST_BANK + n % JOB_BANKS
                    for a in range(HH):
                        last = nc.vector.tensor_scalar(WUT[:, i, b, a], ps[:, bank, a * H:(a + 1) * H],
                                                       vs2[:, b, a:a + 1], None, ALU.mult)
                    last.then_inc(job_dve, 1)
                if job[0] == "m":
                    dve.wait_ge(job_done, n + 1)
                    nc.vector.tensor_copy(Mb[:, job[1]].rearrange("p a o -> p (a o)"),
                                          ps[:, ST_BANK + n % JOB_BANKS]).then_inc(job_dve, 1)
                if job == ("v", TB - 1) or (job[0] == "wu" and n + 1 < len(jobs) and jobs[n + 1][0] == "wu"):
                    _, i, b = jobs[n + 1]
                    dve.wait_ge(dcoef_ready, 2)
                    if job[0] == "wu":
                        dve.wait_ge(job_done, n)
                    for a in range(HH):
                        last = nc.vector.tensor_scalar(Wsc[:, i, a], Wr[:, W + i, a],
                                                       dcoef[:, W + i, b, a:a + 1], None, ALU.mult)
                    last.then_inc(w_scaled, 1)
                for h, i in chunks_after(n):
                    reduce_chunk(h, i, h % 2)
            for i in range(4, CH):
                reduce_chunk(EARLY, i, EARLY % 2)
            with dve.Fori(0, (HEADS - EARLY - 1) // 2) as r:
                for k in range(2):
                    for i in range(CH):
                        reduce_chunk(2 * r + (EARLY + 1 + k), i, k)

            def normalise(groups, tile, k):
                dve.wait_ge(den_loaded, 16 * (k + 1))
                nc.vector.reciprocal(tile, tile).then_inc(rec_ready, 1)
                dve.wait_ge(rd_loaded, 16 * HG * (groups[-1] + 1))
                for i, g in enumerate(groups):
                    nc.vector.tensor_tensor(AT[:, g], AT[:, g], RD[:, i], ALU.mult).then_inc(at_ready, 1)

            def add(t):
                dve.wait_ge(y_done, t + 1)
                if t >= 4:
                    dve.wait_ge(y_stored[t % 4], 16 * (t // 4))
                nc.vector.tensor_tensor(yb[:, t % 4], ps[:, t % 3, 0:H], X[:, t], ALU.add).then_inc(y_added, 1)

            normalise(range(G - 1), den, 0)
            for t in range(TB):
                add(t)
            normalise([G - 1], denl, 1)
            for t in range(TB, NT):
                add(t)

        @block.scalar
        def _(act):
            act.wait_ge(ident_ready, 1)
            nc.scalar.activation(warm[:], identf[:, 0:1], ACT.Exp).then_inc(pv_free, 1)
            act.dma_start(Wr[:, Q], w_in[Q].rearrange("(a p) h -> p a h", p=P)).then_inc(w_loaded[Q], 16)
            act.dma_start(Wr[:, K], w_in[K].rearrange("(a p) h -> p a h", p=P)).then_inc(w_loaded[K], 16)

            def squares(n, w, b):
                act.wait_ge(styled, n + 1)
                for a in range(HH):
                    if n or a:
                        act.wait_ge(squared, HH * n + a)
                    nc.scalar.activation(junk, wsty[:, n % 2, a], ACT.Square,
                                         accum_out=dsum[:, w, b, a:a + 1]).then_inc(squared, 1)

            def copy_mrow(h, hq):
                act.wait_ge(turned, h + 1)
                nc.scalar.copy(mT[:, hq], ps[0:3 * TB, 6 % MAX_BANKS].bitcast(BF16)[:, 0:P]).then_inc(mrow_copied, 1)

            for n, job in enumerate(jobs):
                if n in (3, 7):
                    for k in (range(4) if n == 3 else range(4, 5 * B)):
                        squares(k, k // B, k % B)
                bank = ST_BANK + n % JOB_BANKS
                if job[0] in ("wt", "xt", "qk", "v"):
                    act.wait_ge(job_done, n + 1)
                if job[0] == "wt":
                    nc.scalar.copy(WT[:, job[1]].rearrange("p a o -> p (a o)"), ps[:, bank]).then_inc(job_act, 1)
                if job[0] == "xt":
                    nc.scalar.copy(xT[:, :, job[1] * 2 * P:(job[1] + 1) * 2 * P],
                                   ps[:, bank].rearrange("p (a t) -> p a t", a=HH)).then_inc(job_act, 1)
                if job[0] == "qk":
                    _, g, m, c = job
                    i = qk_index(g, m)
                    act.wait_ge(dcoef_ready, 2)
                    if i >= 2:
                        act.wait_ge(split_rest, 2 * (i - 1))
                        act.wait_ge(stored[i % 2], 48 * (i // 2))
                    col = slice(c * 512, (c + 1) * 512)
                    scale = dcoef[:, m, g // HH, g % HH:g % HH + 1]
                    nc.scalar.activation(full[:, i % 2, col], ps[:, bank], ACT.Copy, scale=scale)
                    nc.scalar.activation(pieces[:, i % 2, 0, col], ps[:, bank], ACT.Copy, scale=scale).then_inc(job_act, 1)
                if job[0] == "v":
                    t = job[1] * 2
                    b = t // TB
                    for a in range(HH):
                        last = nc.scalar.copy(Vall[:, b * HH + a, t % TB:t % TB + 2],
                                              ps[:, bank].rearrange("p (t o) -> p t o", t=2)[:, :, a * P:(a + 1) * P])
                    last.then_inc(job_act, 1)
                for h, i in chunks_after(n):
                    if i == 5 and h:
                        copy_mrow(h - 1, (h - 1) % 4)

            def exps(n, s):
                for hd in range(2):
                    act.wait_ge(st_done, 2 * n + hd + 1)
                    if not isinstance(n, int) or n >= 4:
                        act.wait_ge(pv_done, n - 3)
                    nc.scalar.activation(prob[:, s % 4, hd], ps[:, ST_BANK + 2 * hd:ST_BANK + 2 * hd + 2].rearrange("p c t -> p (c t)"),
                                         ACT.Exp, scale=SCALE).then_inc(exp_done, 1)

            def pair(i, half, p, last_m):
                for s in range(1, STEPS):
                    exps(p * STEPS + s, s)
                    if s == 1 and (last_m is None or 2 * p + 2 <= last_m):
                        copy_mrow(2 * p + 2, (2 * half + 2) % 4)
                    if s == 5 and (last_m is None or 2 * p + 3 <= last_m):
                        copy_mrow(2 * p + 3, (2 * half + 3) % 4)
                if last_m is None or p < PAIRS - 1:
                    exps((p + 1) * STEPS, 0)
                act.wait_ge(pv_done, (p + 1) * STEPS)
                if last_m is None or p >= 2:
                    act.wait_ge(ob_moved[half], 80 * i)
                nc.scalar.copy(ob[:, half], ps[:, PV_BANK]).then_inc(pv_free, 1)

            exps(0, 0)
            for p in range(2):
                pair(0, p, p, HEADS - 1)
            with act.Fori(1, PAIRS // 2 - 1) as i:
                for half in range(2):
                    pair(i, half, 2 * i + half, None)
            for p in (PAIRS - 2, PAIRS - 1):
                pair(p // 2, p % 2, p, HEADS - 1)
            for t in range(NT):
                act.wait_ge(y_added, t + 1)
                act.dma_start(out_v[:, t], yb[:, t % 4]).then_inc(y_stored[t % 4], 16)
            for i in range(4):
                act.wait_ge(y_stored[i], 16 * NT // 4)

        @block.tensor
        def _(pe):
            def form_chunk(h, i, slot, hd, first):
                bank = (i if i < 6 else i + 1) % MAX_BANKS
                if i == 8:
                    if not (isinstance(h, int) and h == 0):
                        pe.wait_ge(mrow_copied, h)
                    else:
                        pe.wait_ge(max_done, 6)
                else:
                    need = {0: -1, 1: 0, 2: -2, 6: 5, 7: 6}.get(i, i - 2)
                    if not first or i >= 3:
                        pe.wait_ge(max_done, h * CH + need)
                qt, kc = divmod(i, C)
                nc.tensor.matmul(ps[:, bank], qst[0:KR, slot, hd, qt * P:(qt + 1) * P],
                                 kst[0:KR, slot, hd, kc * 512:(kc + 1) * 512], start=True, stop=True).then_inc(chunk_done, 1)

            def turn_max(h, hb, own_chunks):
                pe.wait_ge(negmax_split, h + 1)
                pe.wait_ge(max_done, own_chunks)
                nc.tensor.transpose(ps[0:3 * TB, 6 % MAX_BANKS].bitcast(BF16)[:, 0:P],
                                    mpc[:, hb].rearrange("p c t -> p (c t)"), identb[:]).then_inc(turned, 1)

            def chunk(h, i, slot, hd, first=False):
                form_chunk(h, i, slot, hd, first)
                if i == 5 and not first:
                    turn_max(h - 1, 1 - hd, h * CH + 4)

            def stack_ready(g, j):
                pe.wait_ge(stack_loaded[j], 16 * 9 * (g + 1))

            pe.wait_ge(ident_ready, 1)
            for n, job in enumerate(jobs):
                bank = ST_BANK + n % JOB_BANKS
                if n >= JOB_BANKS:
                    emptied(pe, n - JOB_BANKS)
                if job[0] == "wt":
                    w = job[1]
                    pe.wait_ge(w_loaded[w], 16)
                    for a in range(HH):
                        for o in range(HH):
                            last = nc.tensor.transpose(ps[:, bank, a * H + o * P:a * H + (o + 1) * P],
                                                       Wr[:, w, o, a * P:(a + 1) * P], identf[:])
                if job[0] == "xt":
                    t = 2 * job[1]
                    pe.wait_ge(xhat_ready, t + 2)
                    for a in range(HH):
                        for o in range(2):
                            last = nc.tensor.transpose(ps[:, bank, a * H + o * P:a * H + (o + 1) * P],
                                                       xs[:, t + o, a * P:(a + 1) * P], identf[:])
                if job[0] == "qk":
                    _, g, m, c = job
                    b, half = divmod(g, HH)
                    if (m, c) == (Q, 0):
                        emptied(pe, jobs.index(("xt", (b + 1) * TB // 2 - 1)))
                    for a in range(HH):
                        last = nc.tensor.matmul(ps[:, bank], WT[:, m, a, half * P:(half + 1) * P],
                                                xT[:, a, b * S + c * 512:b * S + (c + 1) * 512],
                                                start=(a == 0), stop=(a == HH - 1))
                if job[0] == "v":
                    t = 2 * job[1]
                    for o in range(2):
                        for a in range(HH):
                            last = nc.tensor.matmul(ps[:, bank, o * H:(o + 1) * H], xT[:, a, (t + o) * P:(t + o + 1) * P],
                                                    WT[:, V, a], start=(a == 0), stop=(a == HH - 1))
                if job[0] == "wu":
                    _, i, b = job
                    pe.wait_ge(w_scaled, 2 * b + i + 1)
                    for a in range(HH):
                        for o in range(HH):
                            last = nc.tensor.transpose(ps[:, bank, a * H + o * P:a * H + (o + 1) * P],
                                                       Wsc[:, i, o, a * P:(a + 1) * P], identf[:])
                if job[0] == "m":
                    b = job[1]
                    emptied(pe, jobs.index(("wu", 1, b)))
                    for o in range(HH):
                        for a in range(HH):
                            last = nc.tensor.matmul(ps[:, bank, o * H:(o + 1) * H], Wr[:, V, a, o * P:(o + 1) * P],
                                                    WUT[:, 1, b, a], start=(a == 0), stop=(a == HH - 1))
                last.then_inc(job_done, 1)
                for h, i in chunks_after(n):
                    if i == 0 and h % 2 == 0:
                        if h < 4:
                            stack_ready(0, h // 2)
                    chunk(h, i, h // 2, h % 2, first=(h == 0))

            def half_scores(n, s, slot, hd):
                if not isinstance(n, int) or n >= 1:
                    pe.wait_ge(exp_done, 2 * n + hd - 1)
                for c in range(C):
                    last = nc.tensor.matmul(ps[:, ST_BANK + 2 * hd + c], kst[0:ROWS, slot, hd, s * P:(s + 1) * P],
                                            qst[0:ROWS, slot, hd, c * 512:(c + 1) * 512], start=True, stop=True)
                last.then_inc(st_done, 1)

            def weigh_values(n, s, j):
                pe.wait_ge(exp_done, 2 * n + 2)
                for hd in range(2):
                    for c in range(C):
                        row = 32 * (2 * hd + c)
                        last = nc.tensor.matmul(ps[row:row + VW, PV_BANK], vbuf[:, j, s, hd],
                                                prob[:, s % 4, hd, c * 512:(c + 1) * 512],
                                                start=(s == 0), stop=(s == STEPS - 1), tile_position=(0, row))
                last.then_inc(pv_done, 1)

            def step(g, j, s, final):
                p = g * PG + j
                n = p * STEPS + s
                k = 2 * j + 3 + s // 4
                head_chunks = [(g * HG + k, (k % HG) // 2, k % 2, 4 * (s % 4) + i) for i in range(4)]
                if final and k >= HG:
                    head_chunks = []
                if s == 0:
                    pe.wait_ge(mrow_loaded[j], 96 * (g + 1))
                if s == 4 and head_chunks:
                    stack_ready(g + k // HG, (k % HG) // 2)
                half_scores(n, s, j, 0)
                for h, slot, hd, i in head_chunks[:2]:
                    chunk(h, i, slot, hd)
                half_scores(n, s, j, 1)
                for h, slot, hd, i in head_chunks[2:]:
                    chunk(h, i, slot, hd)
                if final and k == HG and s == 5:
                    turn_max(HEADS - 1, 1, HEADS * CH)
                if s == 1:
                    pe.wait_ge(v_ready, p + 1)
                    pe.wait_ge(pv_free, p + 1)
                if s >= 1:
                    weigh_values(n - 1, s - 1, j)

            def first_step(g, j, final):
                step(g, j, 0, final)
                weigh_values((g * PG + j) * STEPS - 1, STEPS - 1, (j - 1) % PG)

            for n in range(len(jobs) - JOB_BANKS, len(jobs)):
                emptied(pe, n)
            pe.wait_ge(ones_ready, 2)
            pe.wait_ge(mrow_loaded[0], 96)
            half_scores(0, 0, 0, 0)
            half_scores(0, 0, 0, 1)

            def group(g, final):
                for j in range(PG):
                    for s in range(1, STEPS):
                        step(g, j, s, final)
                    if j < PG - 1:
                        first_step(g, j + 1, final)
                    elif not final:
                        first_step(g + 1, 0, False)
                    else:
                        weigh_values(PAIRS * STEPS - 1, STEPS - 1, PG - 1)

            with pe.Fori(0, G - 1) as g:
                group(g, False)
            group(G - 1, True)

            def result(t):
                b = t // TB
                if t >= 3:
                    pe.wait_ge(y_added, t - 2)
                for a in range(HH):
                    nc.tensor.matmul(ps[:, t % 3, 0:H], xT[:, a, t * P:(t + 1) * P], Mb[:, b, a],
                                     start=(a == 0), stop=False)
                for a in range(HH):
                    last = nc.tensor.matmul(ps[:, t % 3, 0:H], AT[:, b * HH + a, (t % TB) * P:(t % TB + 1) * P],
                                            WUT[:, 0, b, a], start=False, stop=(a == HH - 1))
                last.then_inc(y_done, 1)

            pe.wait_ge(at_ready, G - 1)
            for t in range(TB):
                result(t)
            pe.wait_ge(at_ready, G)
            for t in range(TB, NT):
                result(t)


_INS = ["x", "cond_2048", "L0_cond_q_weight", "L0_cond_k_weight", "L0_cond_v_weight", "L0_cond_w_weight",
        "L0_cond_u_weight"]
_OUTS = [((2, 1024, 256), "float32")]


def kernel(**inputs):
    import numpy as _np
    import concourse.bacc as _bacc
    from concourse import mybir as _mybir
    from concourse.bass_utils import run_bass_kernel_spmd as _run

    nc = _bacc.Bacc("TRN2", target_bir_lowering=False, num_devices=1)
    arrays, args = {}, []
    for name in _INS:
        a = _np.ascontiguousarray(inputs[name])
        arrays[f"in_{name}_dram"] = a
        args.append(nc.dram_tensor(f"in_{name}_dram", a.shape, _mybir.dt.from_np(a.dtype), kind="ExternalInput").ap())
    for i, (shape, dtype) in enumerate(_OUTS):
        dt = _mybir.dt.from_np(_np.dtype(dtype))
        args.append(nc.dram_tensor(f"out_{i}_dram", shape, dt, kind="ExternalOutput").ap())
    cond_attention(nc, *args)
    r = _run(nc, [arrays], core_ids=[0])
    got = tuple(r.results[0][f"out_{i}_dram"] for i in range(len(_OUTS)))
    return got[0]
```

```python
from contextlib import ExitStack

import concourse.bass as bass
from concourse import mybir

F32 = mybir.dt.float32
BF16 = mybir.dt.bfloat16
ALU = mybir.AluOpType
ACT = mybir.ActivationFunctionType
AX = mybir.AxisListType

P = 128
NH = 16
Q, K, V, W, U = range(5)
Q_PIECES = (0, 1, 2, 0, 1, 0)
K_PIECES = (0, 0, 0, 1, 1, 2)


def cond_attention(nc: bass.Bass, x, cond, wq, wk, wv, ww, wu, out):
    B, S, H = x.shape
    D = H // NH
    HH = H // P
    TB = S // P
    NT = B * TB
    G = B * HH
    HG = NH // HH
    PG = HG // 2
    PAIRS = G * PG
    HEADS = 2 * PAIRS
    C = S // 512
    KR = len(Q_PIECES) * D
    ROWS = KR + 3
    VW = 2 * D
    STEPS = TB
    CH = TB * C
    EARLY = 3
    RUN = 16 * len(Q_PIECES)
    SCALE = float(D) ** -0.5

    x_v = x.rearrange("b (t p) h -> p (b t) h", p=P)
    out_v = out.rearrange("b (t p) h -> p (b t) h", p=P)
    w_in = (wq, wk, wv, ww, wu)
    piece_dram = [nc.dram_tensor(n, (G, HG, KR // D, D, S), BF16, kind="Internal").ap()
                  for n in ("q_pieces", "k_pieces")]
    den_dram = nc.dram_tensor("denominators", (HEADS, S), F32, kind="Internal").ap()
    rec_dram = nc.dram_tensor("reciprocals", (HEADS, S), F32, kind="Internal").ap()

    with ExitStack() as ctx:
        def sb(name, shape, dt):
            return ctx.enter_context(nc.sbuf_tensor(name, shape, dt))

        def sem(name):
            return ctx.enter_context(nc.semaphore(name))

        ps = ctx.enter_context(nc.psum_tensor("ps", [P, 8, 512], F32))
        MAX_BANKS, ST_BANK, PV_BANK = 3, 3, 7
        JOB_BANKS = 5

        X = sb("X", [P, NT, H], F32)
        xs = sb("xs", [P, NT, H], F32)
        xT = sb("xT", [P, HH, B * S], F32)
        Vall = sb("Vall", [P, G, TB, P], F32)
        prob = sb("prob", [P, 4, 2, S], F32)
        qst = sb("qst", [P, 4, 2, S], BF16)
        kst = sb("kst", [P, 4, 2, S], BF16)
        vbuf = sb("vbuf", [P, PG, TB, 2, VW], F32)
        ob = sb("ob", [P, 2, 512], F32)
        Wr = sb("Wr", [P, 5, HH, H], F32)
        Wsc = sb("Wsc", [P, 2, HH, H], F32)
        WT = sb("WT", [P, 3, HH, H], F32)
        WUT = sb("WUT", [P, 2, B, HH, H], F32)
        Mb = sb("Mb", [P, B, HH, H], F32)
        shared = sb("shared", [P, 7 * S], F32)
        AT = shared[:, 0:G * S].rearrange("p (g t) -> p g t", g=G)
        RD = shared[:, G * S:(G + 3) * S].rearrange("p (g t) -> p g t", g=3)
        full = shared[:, 0:2 * S].rearrange("p (i t) -> p i t", i=2)
        rest = shared[:, 2 * S:4 * S].rearrange("p (i t) -> p i t", i=2)
        pieces = shared[:, 4 * S:7 * S].bitcast(BF16).rearrange("p (i c t) -> p i c t", i=2, c=3)
        wsty = shared[:, 3 * S:3 * S + 2 * HH * H].rearrange("p (i a h) -> p i a h", i=2, a=HH)
        cb = sb("cb", [P, B, 2, H], F32)
        s2col = sb("s2col", [P, B, HH], F32)
        dsum = sb("dsum", [P, 5, B, HH], F32)
        dcoef = sb("dcoef", [P, 5, B, HH], F32)
        vs2 = sb("vs2", [P, B, HH], F32)
        stats = sb("stats", [P, NT, 6], F32)
        mv = sb("mv", [P, NT, 2], F32)
        vareps = sb("vareps", [P, NT], F32)
        rstd = sb("rstd", [P, NT], F32)
        minus_half = sb("minus_half", [P, 5 * G], F32)
        identf = sb("identf", [P, P], F32)
        identb = sb("identb", [P, P], BF16)
        mx = sb("mx", [P, 2, TB, C], F32)
        nm = sb("nm", [P, 2, TB], F32)
        nmr = sb("nmr", [P, 2, 2, TB], F32)
        mpc = sb("mpc", [P, 2, 3, TB], BF16)
        mT = sb("mT", [3 * TB, 4, P], BF16)
        junk = shared[:, 2 * S:2 * S + H]
        denf = xs[:, 4, 0:S * (HEADS - 4) // P]
        denl = xs[:, 5, 0:S * 2 // P]
        rlast = xs[:, 6:8].rearrange("p a h -> p (a h)")
        yb = xs[:, 0:4]

        warm = sb("warm", [P, 1], F32)
        zeros = sb("zeros", [P, TB], F32)

        x_loaded = [sem(f"x_loaded{b}") for b in range(B)]
        w_loaded = [sem(f"w_loaded{w}") for w in range(5)]
        cond_loaded, s2_loaded = sem("cond_loaded"), sem("s2_loaded")
        ident_ready, consts_ready, pool_own = sem("ident_ready"), sem("consts_ready"), sem("pool_own")
        styled, squared = sem("styled"), sem("squared")
        dcoef_ready, vs2_ready = sem("dcoef_ready"), sem("vs2_ready")
        dve_own, var_ready, rstd_ready, xhat_ready = sem("dve_own"), sem("var_ready"), sem("rstd_ready"), sem("xhat_ready")
        w_scaled = sem("w_scaled")
        job_done, job_act, job_dve = sem("job_done"), sem("job_act"), sem("job_dve")
        split_rest, split_last = sem("split_rest"), sem("split_last")
        stored = [sem(f"stored{i}") for i in range(2)]
        stack_loaded = [sem(f"stack_loaded{i}") for i in range(4)]
        chunk_done, max_done, negmax_ready = sem("chunk_done"), sem("max_done"), sem("negmax_ready")
        negmax_split, msplit_own = sem("negmax_split"), sem("msplit_own")
        turned, mrow_copied = sem("turned"), sem("mrow_copied")
        mrow_loaded = [sem(f"mrow_loaded{i}") for i in range(4)]
        st_done, exp_done, pv_done = sem("st_done"), sem("exp_done"), sem("pv_done")
        v_ready, pv_free = sem("v_ready"), sem("pv_free")
        ob_moved = [sem(f"ob_moved{i}") for i in range(2)]
        ones_ready = sem("ones_ready")
        den_loaded, rec_ready, rec_stored, rd_loaded, at_ready = (
            sem("den_loaded"), sem("rec_ready"), sem("rec_stored"), sem("rd_loaded"), sem("at_ready"))
        rd_last, split_second, dcoef_own = sem("rd_last"), sem("split_second"), sem("dcoef_own")
        y_done, y_added = sem("y_done"), sem("y_added")
        y_stored = [sem(f"y_stored{i}") for i in range(4)]

        jobs = [("wt", w) for w in (Q, K, V)]
        jobs += [("xt", t) for t in range(TB // 2)]
        jobs += [("qk", 0, m, c) for m in (Q, K) for c in range(C)]
        jobs += [("xt", t) for t in range(TB // 2, TB)]
        jobs += [("qk", 1, m, c) for m in (Q, K) for c in range(C)]
        jobs += [("v", t) for t in range(TB // 2)]
        jobs += [("qk", g, m, c) for g in (2, 3) for m in (Q, K) for c in range(C)]
        jobs += [("v", t) for t in range(TB // 2, TB)]
        jobs += [("wu", i, b) for b in range(B) for i in range(2)]
        jobs += [("m", b) for b in range(B)]
        on_dve = [j[0] in ("wu", "m") for j in jobs]
        FIRST_CHUNK = 21

        def chunks_after(n):
            last = len(jobs) - 1
            if n < FIRST_CHUNK:
                return []
            total, at = EARLY * CH + 4, 3 * (n - FIRST_CHUNK)
            return [divmod(i, CH) for i in range(min(at, total), total if n == last else min(at + 3, total))]

        def emptied(eng, n):
            count = sum(d == on_dve[n] for d in on_dve[:n + 1])
            eng.wait_ge(job_dve if on_dve[n] else job_act, count)

        def qk_index(g, m):
            return 2 * g + m

        LAST_BANKS = (3, 4, 5, 6, 7, 0, 1, 2)

        block = ctx.enter_context(nc.Block())

        @block.sync
        def _(sp):
            sp.dma_start(cb[:, 0], cond[0].rearrange("(s h) -> s h", s=2).partition_broadcast(P)).then_inc(cond_loaded, 16)
            sp.dma_start(cb[:, 1], cond[1].rearrange("(s h) -> s h", s=2).partition_broadcast(P)).then_inc(cond_loaded, 16)
            for t in range(0, TB, TB // 2):
                sp.dma_start(X[:, t:t + TB // 2], x_v[:, t:t + TB // 2]).then_inc(x_loaded[0], 16)
            for w in (V, W, U):
                sp.dma_start(Wr[:, w], w_in[w].rearrange("(a p) h -> p a h", p=P)).then_inc(w_loaded[w], 16)
            for b in range(B):
                with nc.allow_non_contiguous_dma(reason="one style for each partition"):
                    sp.dma_start(s2col[:, b], cond[b, H:2 * H].rearrange("(a p) -> p a", p=P)).then_inc(s2_loaded, 16)
            for t in range(TB, NT, TB // 2):
                sp.dma_start(X[:, t:t + TB // 2], x_v[:, t:t + TB // 2]).then_inc(x_loaded[1], 16)

            def store_pieces(g, m):
                i = qk_index(g, m)
                for run, c in sorted(enumerate((Q_PIECES, K_PIECES)[m]), key=lambda rc: rc[1]):
                    if c == 0:
                        emptied(sp, jobs.index(("qk", g, m, C - 1)))
                    elif c == 1:
                        sp.wait_ge(split_second, i + 1)
                    else:
                        sp.wait_ge(split_last, i + 1)
                    sp.dma_start(piece_dram[m][g, :, run], pieces[:, i % 2, c]).then_inc(stored[i % 2], 16)

            def load_stacks(g, j):
                for m, stack in ((Q, qst), (K, kst)):
                    sp.dma_start(stack[0:KR, j], piece_dram[m][g, 2 * j:2 * j + 2].rearrange("h c d t -> (c d) h t")
                                 ).then_inc(stack_loaded[j], 16)

            def move_mrow(h, hg):
                sp.wait_ge(mrow_copied, h + 1)
                sp.dma_start(qst[KR:ROWS, hg // 2, hg % 2].rearrange("c (a t) -> c a t", a=TB),
                             mT[:, hg % 4]).then_inc(mrow_loaded[hg // 2], 16)

            def move_output(g, j):
                sp.wait_ge(pv_free, g * PG + j + 2)
                for hd in range(2):
                    for c in range(C):
                        row = 32 * (2 * hd + c)
                        sp.dma_start(AT[(2 * j + hd) * D:(2 * j + hd + 1) * D, g, c * 512:(c + 1) * 512],
                                     ob[row:row + D, j % 2]).then_inc(ob_moved[j % 2], 16)
                sp.dma_start(den_dram[bass.ds(g * HG + 2 * j, 2)].rearrange("h (c t) -> (h c) t", c=C),
                             ob[D:P:32, j % 2]).then_inc(ob_moved[j % 2], 16)

            for g in range(G):
                for m in (Q, K):
                    store_pieces(g, m)
                if g == 0:
                    sp.wait_ge(stored[0], RUN)
                    sp.wait_ge(stored[1], RUN)
                    load_stacks(0, 0)
                    load_stacks(0, 1)
            move_mrow(0, 0)
            move_mrow(1, 1)
            for i in range(2):
                sp.wait_ge(stored[i], RUN * G)

            def rows(g, j):
                p = g * PG + j
                move_mrow(2 * p + 2, (2 * j + 2) % HG)
                move_mrow(2 * p + 3, (2 * j + 3) % HG)

            def pair(g, j):
                p = g * PG + j
                rows(g, j)
                sp.wait_ge(st_done, 2 * STEPS * (p + 1) + 1)
                load_stacks(g + (j + 3) // PG, (j + 3) % PG)
                move_output(g, j)

            sp.wait_ge(st_done, 1)
            load_stacks(0, 2)
            with sp.Fori(0, G - 1) as g:
                for j in range(PG):
                    pair(g, j)

            def reciprocals(h0, n, tile, k):
                flat = den_dram[h0:h0 + n].rearrange("h t -> (h t)").rearrange("(p f) -> p f", p=P)
                back = rec_dram[h0:h0 + n].rearrange("h t -> (h t)").rearrange("(p f) -> p f", p=P)
                sp.dma_start(tile, flat).then_inc(den_loaded, 16)
                sp.wait_ge(rec_ready, k + 1)
                sp.dma_start(back, tile).then_inc(rec_stored, 16)
                sp.wait_ge(rec_stored, 16 * (k + 1))

            def spread(h, n, slot):
                sp.dma_start(RD[h % HG * D:(h % HG + n) * D, slot],
                             rec_dram[h:h + n].unsqueeze(1).to_broadcast([n, D, S])).then_inc(rd_loaded, 16)

            rows(G - 1, 0)
            sp.wait_ge(st_done, 2 * STEPS * ((G - 1) * PG + 1) + 1)
            load_stacks(G - 1, 3)
            move_output(G - 1, 0)
            rows(G - 1, 1)
            move_output(G - 1, 1)
            for i in range(2):
                sp.wait_ge(ob_moved[i], 16 * 5 * (2 * G - 1))
            rows(G - 1, 2)
            reciprocals(0, HEADS - 4, denf, 0)
            for g in range(G - 1):
                spread(g * HG, HG, g)
            move_output(G - 1, 2)
            sp.wait_ge(ob_moved[0], 16 * 5 * 2 * G)
            reciprocals(HEADS - 4, 2, denl, 1)
            sp.wait_ge(at_ready, 1)
            spread((G - 1) * HG, 6, 0)
            move_output(G - 1, 3)
            sp.wait_ge(rec_ready, 3)
            for hd in range(2):
                for c in range(C):
                    row = 32 * (2 * hd + c) + D
                    sp.dma_start(RD[(6 + hd) * D:(7 + hd) * D, 0, c * 512:(c + 1) * 512],
                                 rlast[row:row + D]).then_inc(rd_last, 16)

        @block.gpsimd
        def _(pool):
            own = 0
            nc.gpsimd.memset(identf[:], 0.0).then_inc(pool_own, 1)
            nc.gpsimd.memset(zeros[:], 0.0)
            nc.gpsimd.memset(minus_half[:], -0.5).then_inc(pool_own, 1)
            pool.wait_ge(pool_own, 2)
            nc.gpsimd.affine_select(out=identf[:], in_=identf[:], compare_op=ALU.not_equal, fill=1.0, base=0,
                                    pattern=[[-1, P]], channel_multiplier=1).then_inc(pool_own, 1)
            pool.wait_ge(pool_own, 3)
            nc.gpsimd.tensor_copy(identb[:], identf[:]).then_inc(ident_ready, 1)
            pool.wait_ge(ident_ready, 1)
            nc.gpsimd.memset(kst[KR:ROWS], 1.0).then_inc(ones_ready, 1)
            pool.wait_ge(ones_ready, 1)
            nc.gpsimd.memset(vbuf[:], 1.0).then_inc(ones_ready, 1)

            def inverse_roots(b):
                t = slice(b * TB, (b + 1) * TB)
                pool.wait_ge(var_ready, b + 1)
                nc.gpsimd.tensor_scalar(vareps[:, t], mv[:, t, 1], 1e-5, None, ALU.add).then_inc(pool_own, 1)
                pool.wait_ge(pool_own, 4 + b)
                nc.gpsimd.tensor_tensor(rstd[:, t], vareps[:, t], minus_half[:, 0:TB], ALU.pow).then_inc(rstd_ready, 1)

            def demodulate(w0, n, k):
                at = slice(w0, w0 + n)
                sums, roots = (a[:, at].rearrange("p w b a -> p (w b a)") for a in (dsum, dcoef))
                pool.wait_ge(squared, G * (w0 + n))
                nc.gpsimd.tensor_scalar(sums, sums, 1e-8, None, ALU.add).then_inc(dcoef_own, 1)
                pool.wait_ge(dcoef_own, k + 1)
                nc.gpsimd.tensor_tensor(roots, sums, minus_half[:, 0:G * n], ALU.pow).then_inc(dcoef_ready, 1)

            demodulate(Q, 2, 0)
            inverse_roots(0)
            demodulate(V, 3, 1)
            pool.wait_ge(dcoef_ready, 2)
            pool.wait_ge(s2_loaded, 32)
            nc.gpsimd.tensor_tensor(vs2[:].rearrange("p b a -> p (b a)"), dcoef[:, V].rearrange("p b a -> p (b a)"),
                                    s2col[:].rearrange("p b a -> p (b a)"), ALU.mult).then_inc(vs2_ready, 1)
            inverse_roots(1)

            def split_max(h, hb):
                pool.wait_ge(negmax_ready, h + 1)
                nc.gpsimd.tensor_tensor(mpc[:, hb, 0], nm[:, hb], zeros[:], ALU.add).then_inc(msplit_own, 1)
                pool.wait_ge(msplit_own, 4 * h + 1)
                nc.gpsimd.tensor_tensor(nmr[:, hb, 0], nm[:, hb], mpc[:, hb, 0], ALU.subtract).then_inc(msplit_own, 1)
                pool.wait_ge(msplit_own, 4 * h + 2)
                nc.gpsimd.tensor_tensor(mpc[:, hb, 1], nmr[:, hb, 0], zeros[:], ALU.add).then_inc(msplit_own, 1)
                pool.wait_ge(msplit_own, 4 * h + 3)
                nc.gpsimd.tensor_tensor(nmr[:, hb, 1], nmr[:, hb, 0], mpc[:, hb, 1], ALU.subtract).then_inc(msplit_own, 1)
                pool.wait_ge(msplit_own, 4 * h + 4)
                nc.gpsimd.tensor_tensor(mpc[:, hb, 2], nmr[:, hb, 1], zeros[:], ALU.add).then_inc(negmax_split, 1)

            def values(g, j):
                nc.gpsimd.tensor_copy(vbuf[:, j, :, :, 0:D],
                                      Vall[:, g, :, 2 * j * D:2 * (j + 1) * D].rearrange("p t (h d) -> p t h d", h=2)
                                      ).then_inc(v_ready, 1)

            for n, job in enumerate(jobs):
                if job[0] == "qk" and job[3] == C - 1:
                    i = qk_index(job[1], job[2])
                    pool.wait_ge(split_second, i + 1)
                    nc.gpsimd.tensor_tensor(pieces[:, i % 2, 2], rest[:, i % 2], pieces[:, i % 2, 1],
                                            ALU.subtract).then_inc(split_last, 1)
                if job == ("v", TB // 2 - 1):
                    emptied(pool, n)
                    pool.wait_ge(ones_ready, 2)
                    values(0, 0)
                for h, i in chunks_after(n):
                    if i == CH - 1:
                        split_max(h, h % 2)

            emptied(pool, jobs.index(("v", TB - 1)))

            with pool.Fori(0, G - 1) as g:
                for j in range(PG):
                    p = g * PG + j
                    split_max(2 * p + 3, 1)
                    values(g + (j + 1) // PG, (j + 1) % PG)
                    split_max(2 * p + 4, 0)
            for j in range(PG - 1):
                p = (G - 1) * PG + j
                if 2 * p + 3 < HEADS:
                    split_max(2 * p + 3, 1)
                values(G - 1, j + 1)
                if 2 * p + 4 < HEADS:
                    split_max(2 * p + 4, 0)

        @block.vector
        def _(dve):
            own = [0]

            def after(ins):
                own[0] += 1
                ins.then_inc(dve_own, 1)
                dve.wait_ge(dve_own, own[0])

            def norm_stats(b):
                t = slice(b * TB, (b + 1) * TB)
                dve.wait_ge(x_loaded[b], 32)
                after(nc.vector.tensor_tensor(xs[:, t], X[:, t], cb[:, b, 0:1].to_broadcast([P, TB, H]), ALU.mult))
                for i in range(b * TB, (b + 1) * TB):
                    last = nc.vector.bn_stats(stats[:, i], xs[:, i])
                after(last)
                for i in range(b * TB, (b + 1) * TB):
                    last = nc.vector.bn_aggr(mv[:, i], stats[:, i])
                last.then_inc(var_ready, 1)

            def norm_apply(b):
                dve.wait_ge(rstd_ready, b + 1)
                for i in range(b * TB, (b + 1) * TB):
                    nc.vector.tensor_scalar(xs[:, i], xs[:, i], mv[:, i, 0:1], rstd[:, i:i + 1],
                                            ALU.subtract, ALU.mult).then_inc(xhat_ready, 1)

            def style(n, w, b):
                dve.wait_ge(w_loaded[w], 16)
                if n >= 2:
                    dve.wait_ge(squared, HH * (n - 1))
                part = 0 if w in (Q, K, V) else 1
                nc.vector.tensor_tensor(wsty[:, n % 2], Wr[:, w], cb[:, b, part:part + 1].to_broadcast([P, HH, H]),
                                        ALU.mult).then_inc(styled, 1)

            dve.wait_ge(cond_loaded, 32)
            for n in range(2 * B):
                style(n, n // B, n % B)
            norm_stats(0)
            for n in range(2 * B, 4 * B):
                style(n, n // B, n % B)
            norm_apply(0)
            for n in range(4 * B, 5 * B):
                style(n, n // B, n % B)
            norm_stats(1)
            norm_apply(1)

            def reduce_chunk(h, i, hb):
                bank = (i if i < 6 else i + 1) % MAX_BANKS
                dve.wait_ge(chunk_done, h * CH + i + 1)
                nc.vector.tensor_reduce(mx[:, hb, i // C, i % C:i % C + 1], ps[:, bank], AX.X, ALU.max).then_inc(max_done, 1)
                if i == CH - 1:
                    dve.wait_ge(max_done, (h + 1) * CH)
                    nc.vector.tensor_reduce(nm[:, hb], mx[:, hb], AX.X, ALU.max, negate=True).then_inc(negmax_ready, 1)

            for n, job in enumerate(jobs):
                if job[0] == "qk" and job[3] == C - 1:
                    i = qk_index(job[1], job[2])
                    emptied(dve, n)
                    if i >= 2:
                        dve.wait_ge(split_last, i - 1)
                    nc.vector.tensor_tensor(rest[:, i % 2], full[:, i % 2], pieces[:, i % 2, 0],
                                            ALU.subtract).then_inc(split_rest, 1)
                if job[0] == "wu":
                    _, i, b = job
                    dve.wait_ge(job_done, n + 1)
                    dve.wait_ge(vs2_ready, 1)
                    bank = ST_BANK + n % JOB_BANKS
                    for a in range(HH):
                        last = nc.vector.tensor_scalar(WUT[:, i, b, a], ps[:, bank, a * H:(a + 1) * H],
                                                       vs2[:, b, a:a + 1], None, ALU.mult)
                    last.then_inc(job_dve, 1)
                if job[0] == "m":
                    dve.wait_ge(job_done, n + 1)
                    nc.vector.tensor_copy(Mb[:, job[1]].rearrange("p a o -> p (a o)"),
                                          ps[:, ST_BANK + n % JOB_BANKS]).then_inc(job_dve, 1)
                if job == ("v", TB - 1) or (job[0] == "wu" and n + 1 < len(jobs) and jobs[n + 1][0] == "wu"):
                    _, i, b = jobs[n + 1]
                    dve.wait_ge(dcoef_ready, 2)
                    if job[0] == "wu":
                        dve.wait_ge(job_done, n)
                    for a in range(HH):
                        last = nc.vector.tensor_scalar(Wsc[:, i, a], Wr[:, W + i, a],
                                                       dcoef[:, W + i, b, a:a + 1], None, ALU.mult)
                    last.then_inc(w_scaled, 1)
                for h, i in chunks_after(n):
                    reduce_chunk(h, i, h % 2)
            for i in range(4, CH):
                reduce_chunk(EARLY, i, EARLY % 2)
            with dve.Fori(0, (HEADS - EARLY - 1) // 2) as r:
                for k in range(2):
                    for i in range(CH):
                        reduce_chunk(2 * r + (EARLY + 1 + k), i, k)

            def add(t, bank):
                dve.wait_ge(y_done, t + 1)
                if t >= 4:
                    dve.wait_ge(y_stored[t % 4], 16 * (t // 4))
                nc.vector.tensor_tensor(yb[:, t % 4], ps[:, bank, 0:H], X[:, t], ALU.add).then_inc(y_added, 1)

            dve.wait_ge(den_loaded, 16)
            nc.vector.reciprocal(denf, denf).then_inc(rec_ready, 1)
            for g in range(G - 1):
                dve.wait_ge(rd_loaded, 16 * (G - 1))
                nc.vector.tensor_tensor(AT[:, g], AT[:, g], RD[:, g], ALU.mult).then_inc(at_ready, 1)
            dve.wait_ge(den_loaded, 32)
            nc.vector.reciprocal(denl, denl).then_inc(rec_ready, 1)
            dve.wait_ge(pv_free, PAIRS + 1)
            nc.vector.reciprocal(rlast, ob[:, (PAIRS - 1) % 2]).then_inc(rec_ready, 1)
            for t in range(TB):
                add(t, t % 3)
            dve.wait_ge(rd_loaded, 16 * G)
            dve.wait_ge(rd_last, 64)
            for i in range(2):
                dve.wait_ge(ob_moved[i], 80 * 2 * G)
            nc.vector.tensor_tensor(AT[:, G - 1], AT[:, G - 1], RD[:, 0], ALU.mult).then_inc(at_ready, 1)
            for t in range(TB, NT):
                add(t, LAST_BANKS[t - TB])

        @block.scalar
        def _(act):
            act.wait_ge(ident_ready, 1)
            nc.scalar.activation(warm[:], identf[:, 0:1], ACT.Exp).then_inc(pv_free, 1)
            act.dma_start(Wr[:, Q], w_in[Q].rearrange("(a p) h -> p a h", p=P)).then_inc(w_loaded[Q], 16)
            act.dma_start(Wr[:, K], w_in[K].rearrange("(a p) h -> p a h", p=P)).then_inc(w_loaded[K], 16)

            def squares(n, w, b):
                act.wait_ge(styled, n + 1)
                for a in range(HH):
                    if n or a:
                        act.wait_ge(squared, HH * n + a)
                    nc.scalar.activation(junk, wsty[:, n % 2, a], ACT.Square,
                                         accum_out=dsum[:, w, b, a:a + 1]).then_inc(squared, 1)

            def copy_mrow(h, hq):
                act.wait_ge(turned, h + 1)
                nc.scalar.copy(mT[:, hq], ps[0:3 * TB, 6 % MAX_BANKS].bitcast(BF16)[:, 0:P]).then_inc(mrow_copied, 1)

            for n, job in enumerate(jobs):
                for k in {0: range(2 * B), 3: range(2 * B, 4 * B), 7: range(4 * B, 5 * B)}.get(n, ()):
                    squares(k, k // B, k % B)
                bank = ST_BANK + n % JOB_BANKS
                if job[0] in ("wt", "xt", "qk", "v"):
                    act.wait_ge(job_done, n + 1)
                if job[0] == "wt":
                    nc.scalar.copy(WT[:, job[1]].rearrange("p a o -> p (a o)"), ps[:, bank]).then_inc(job_act, 1)
                if job[0] == "xt":
                    nc.scalar.copy(xT[:, :, job[1] * 2 * P:(job[1] + 1) * 2 * P],
                                   ps[:, bank].rearrange("p (a t) -> p a t", a=HH)).then_inc(job_act, 1)
                if job[0] == "qk":
                    _, g, m, c = job
                    i = qk_index(g, m)
                    act.wait_ge(dcoef_ready, 1)
                    if i >= 2:
                        act.wait_ge(split_rest, i - 1)
                        act.wait_ge(stored[i % 2], RUN * (i // 2))
                    col = slice(c * 512, (c + 1) * 512)
                    scale = dcoef[:, m, g // HH, g % HH:g % HH + 1]
                    nc.scalar.activation(full[:, i % 2, col], ps[:, bank], ACT.Copy, scale=scale)
                    nc.scalar.activation(pieces[:, i % 2, 0, col], ps[:, bank], ACT.Copy, scale=scale).then_inc(job_act, 1)
                if job[0] == "v":
                    t = job[1] * 2
                    b = t // TB
                    for a in range(HH):
                        last = nc.scalar.copy(Vall[:, b * HH + a, t % TB:t % TB + 2],
                                              ps[:, bank].rearrange("p (t o) -> p t o", t=2)[:, :, a * P:(a + 1) * P])
                    last.then_inc(job_act, 1)
                if n and jobs[n - 1][0] == "qk" and jobs[n - 1][3] == C - 1:
                    i = qk_index(jobs[n - 1][1], jobs[n - 1][2])
                    act.wait_ge(split_rest, i + 1)
                    nc.scalar.copy(pieces[:, i % 2, 1], rest[:, i % 2]).then_inc(split_second, 1)
                for h, i in chunks_after(n):
                    if i == 5 and h:
                        copy_mrow(h - 1, (h - 1) % 4)

            def exps(n, s):
                for hd in range(2):
                    act.wait_ge(st_done, 2 * n + hd + 1)
                    if not isinstance(n, int) or n >= 4:
                        act.wait_ge(pv_done, n - 3)
                    nc.scalar.activation(prob[:, s % 4, hd], ps[:, ST_BANK + 2 * hd:ST_BANK + 2 * hd + 2].rearrange("p c t -> p (c t)"),
                                         ACT.Exp, scale=SCALE).then_inc(exp_done, 1)

            def pair(i, half, p, last_m):
                for s in range(1, STEPS):
                    exps(p * STEPS + s, s)
                    if s == 1 and (last_m is None or 2 * p + 2 <= last_m):
                        copy_mrow(2 * p + 2, (2 * half + 2) % 4)
                    if s == 5 and (last_m is None or 2 * p + 3 <= last_m):
                        copy_mrow(2 * p + 3, (2 * half + 3) % 4)
                if last_m is None or p < PAIRS - 1:
                    exps((p + 1) * STEPS, 0)
                act.wait_ge(pv_done, (p + 1) * STEPS)
                if last_m is None or p >= 2:
                    act.wait_ge(ob_moved[half], 80 * i)
                nc.scalar.copy(ob[:, half], ps[:, PV_BANK]).then_inc(pv_free, 1)

            exps(0, 0)
            for p in range(2):
                pair(0, p, p, HEADS - 1)
            with act.Fori(1, PAIRS // 2 - 1) as i:
                for half in range(2):
                    pair(i, half, 2 * i + half, None)
            for p in (PAIRS - 2, PAIRS - 1):
                pair(p // 2, p % 2, p, HEADS - 1)
            for t in range(NT):
                act.wait_ge(y_added, t + 1)
                act.dma_start(out_v[:, t], yb[:, t % 4]).then_inc(y_stored[t % 4], 16)
            for i in range(4):
                act.wait_ge(y_stored[i], 16 * NT // 4)

        @block.tensor
        def _(pe):
            def form_chunk(h, i, slot, hd, first):
                bank = (i if i < 6 else i + 1) % MAX_BANKS
                if i == 8:
                    if not (isinstance(h, int) and h == 0):
                        pe.wait_ge(mrow_copied, h)
                    else:
                        pe.wait_ge(max_done, 6)
                else:
                    need = {0: -1, 1: 0, 2: -2, 6: 5, 7: 6}.get(i, i - 2)
                    if not first or i >= 3:
                        pe.wait_ge(max_done, h * CH + need)
                qt, kc = divmod(i, C)
                nc.tensor.matmul(ps[:, bank], qst[0:KR, slot, hd, qt * P:(qt + 1) * P],
                                 kst[0:KR, slot, hd, kc * 512:(kc + 1) * 512], start=True, stop=True).then_inc(chunk_done, 1)

            def turn_max(h, hb, own_chunks):
                pe.wait_ge(negmax_split, h + 1)
                pe.wait_ge(max_done, own_chunks)
                nc.tensor.transpose(ps[0:3 * TB, 6 % MAX_BANKS].bitcast(BF16)[:, 0:P],
                                    mpc[:, hb].rearrange("p c t -> p (c t)"), identb[:]).then_inc(turned, 1)

            def chunk(h, i, slot, hd, first=False):
                form_chunk(h, i, slot, hd, first)
                if i == 5 and not first:
                    turn_max(h - 1, 1 - hd, h * CH + 4)

            def stack_ready(g, j):
                pe.wait_ge(stack_loaded[j], 32 * (g + 1))

            pe.wait_ge(ident_ready, 1)
            for n, job in enumerate(jobs):
                bank = ST_BANK + n % JOB_BANKS
                if n >= JOB_BANKS:
                    emptied(pe, n - JOB_BANKS)
                if job[0] == "wt":
                    w = job[1]
                    pe.wait_ge(w_loaded[w], 16)
                    for a in range(HH):
                        for o in range(HH):
                            last = nc.tensor.transpose(ps[:, bank, a * H + o * P:a * H + (o + 1) * P],
                                                       Wr[:, w, o, a * P:(a + 1) * P], identf[:])
                if job[0] == "xt":
                    t = 2 * job[1]
                    pe.wait_ge(xhat_ready, t + 2)
                    for a in range(HH):
                        for o in range(2):
                            last = nc.tensor.transpose(ps[:, bank, a * H + o * P:a * H + (o + 1) * P],
                                                       xs[:, t + o, a * P:(a + 1) * P], identf[:])
                if job[0] == "qk":
                    _, g, m, c = job
                    b, half = divmod(g, HH)
                    if (m, c) == (Q, 0):
                        emptied(pe, jobs.index(("xt", (b + 1) * TB // 2 - 1)))
                    for a in range(HH):
                        last = nc.tensor.matmul(ps[:, bank], WT[:, m, a, half * P:(half + 1) * P],
                                                xT[:, a, b * S + c * 512:b * S + (c + 1) * 512],
                                                start=(a == 0), stop=(a == HH - 1))
                if job[0] == "v":
                    t = 2 * job[1]
                    for o in range(2):
                        for a in range(HH):
                            last = nc.tensor.matmul(ps[:, bank, o * H:(o + 1) * H], xT[:, a, (t + o) * P:(t + o + 1) * P],
                                                    WT[:, V, a], start=(a == 0), stop=(a == HH - 1))
                if job[0] == "wu":
                    _, i, b = job
                    pe.wait_ge(w_scaled, 2 * b + i + 1)
                    for a in range(HH):
                        for o in range(HH):
                            last = nc.tensor.transpose(ps[:, bank, a * H + o * P:a * H + (o + 1) * P],
                                                       Wsc[:, i, o, a * P:(a + 1) * P], identf[:])
                if job[0] == "m":
                    b = job[1]
                    emptied(pe, jobs.index(("wu", 1, b)))
                    for o in range(HH):
                        for a in range(HH):
                            last = nc.tensor.matmul(ps[:, bank, o * H:(o + 1) * H], Wr[:, V, a, o * P:(o + 1) * P],
                                                    WUT[:, 1, b, a], start=(a == 0), stop=(a == HH - 1))
                last.then_inc(job_done, 1)
                for h, i in chunks_after(n):
                    if i == 0 and h % 2 == 0:
                        if h < 4:
                            stack_ready(0, h // 2)
                    chunk(h, i, h // 2, h % 2, first=(h == 0))

            def half_scores(n, s, slot, hd):
                if not isinstance(n, int) or n >= 1:
                    pe.wait_ge(exp_done, 2 * n + hd - 1)
                for c in range(C):
                    last = nc.tensor.matmul(ps[:, ST_BANK + 2 * hd + c], kst[0:ROWS, slot, hd, s * P:(s + 1) * P],
                                            qst[0:ROWS, slot, hd, c * 512:(c + 1) * 512], start=True, stop=True)
                last.then_inc(st_done, 1)

            def weigh_values(n, s, j):
                pe.wait_ge(exp_done, 2 * n + 2)
                for hd in range(2):
                    for c in range(C):
                        row = 32 * (2 * hd + c)
                        last = nc.tensor.matmul(ps[row:row + VW, PV_BANK], vbuf[:, j, s, hd],
                                                prob[:, s % 4, hd, c * 512:(c + 1) * 512],
                                                start=(s == 0), stop=(s == STEPS - 1), tile_position=(0, row))
                last.then_inc(pv_done, 1)

            def step(g, j, s, final):
                p = g * PG + j
                n = p * STEPS + s
                k = 2 * j + 3 + s // 4
                head_chunks = [(g * HG + k, (k % HG) // 2, k % 2, 4 * (s % 4) + i) for i in range(4)]
                if final and k >= HG:
                    head_chunks = []
                if s == 0:
                    pe.wait_ge(mrow_loaded[j], 32 * (g + 1))
                if s == 4 and head_chunks:
                    stack_ready(g + k // HG, (k % HG) // 2)
                half_scores(n, s, j, 0)
                for h, slot, hd, i in head_chunks[:1]:
                    chunk(h, i, slot, hd)
                half_scores(n, s, j, 1)
                for h, slot, hd, i in head_chunks[1:3]:
                    chunk(h, i, slot, hd)
                if final and k == HG and s == 5:
                    turn_max(HEADS - 1, 1, HEADS * CH)
                if s == 1:
                    pe.wait_ge(v_ready, p + 1)
                    pe.wait_ge(pv_free, p + 1)
                if s >= 1:
                    weigh_values(n - 1, s - 1, j)
                elif not (isinstance(p, int) and p == 0):
                    weigh_values(n - 1, STEPS - 1, (j - 1) % PG)
                for h, slot, hd, i in head_chunks[3:]:
                    chunk(h, i, slot, hd)

            for n in range(len(jobs) - JOB_BANKS, len(jobs)):
                emptied(pe, n)
            pe.wait_ge(ones_ready, 2)
            pe.wait_ge(mrow_loaded[0], 32)
            half_scores(0, 0, 0, 0)
            half_scores(0, 0, 0, 1)

            def group(g, final):
                for j in range(PG):
                    for s in range(1, STEPS):
                        step(g, j, s, final)
                    if j < PG - 1:
                        step(g, j + 1, 0, final)
                    elif not final:
                        step(g + 1, 0, 0, False)
                    else:
                        weigh_values(PAIRS * STEPS - 1, STEPS - 1, PG - 1)

            with pe.Fori(0, G - 1) as g:
                group(g, False)
            group(G - 1, True)

            def part(t, bank, chunks):
                b = t // TB
                for a in chunks:
                    if a < HH:
                        left, right = xT[:, a, t * P:(t + 1) * P], Mb[:, b, a]
                    else:
                        left, right = AT[:, b * HH + a - HH, (t % TB) * P:(t % TB + 1) * P], WUT[:, 0, b, a - HH]
                    last = nc.tensor.matmul(ps[:, bank, 0:H], left, right, start=(a == 0), stop=(a == 2 * HH - 1))
                return last

            pe.wait_ge(at_ready, G - 1)
            for t in range(TB):
                if t >= 3:
                    pe.wait_ge(y_added, t - 2)
                part(t, t % 3, range(2 * HH)).then_inc(y_done, 1)
            pe.wait_ge(pv_free, PAIRS + 1)
            for i, bank in enumerate(LAST_BANKS):
                if bank < 3:
                    pe.wait_ge(y_added, TB)
                part(TB + i, bank, range(2 * HH - 1))
            pe.wait_ge(at_ready, G)
            for i, bank in enumerate(LAST_BANKS):
                part(TB + i, bank, [2 * HH - 1]).then_inc(y_done, 1)


_INS = ["x", "cond_2048", "L0_cond_q_weight", "L0_cond_k_weight", "L0_cond_v_weight", "L0_cond_w_weight",
        "L0_cond_u_weight"]
_OUTS = [((2, 1024, 256), "float32")]


def kernel(**inputs):
    import numpy as _np
    import concourse.bacc as _bacc
    from concourse import mybir as _mybir
    from concourse.bass_utils import run_bass_kernel_spmd as _run

    nc = _bacc.Bacc("TRN2", target_bir_lowering=False, num_devices=1)
    arrays, args = {}, []
    for name in _INS:
        a = _np.ascontiguousarray(inputs[name])
        arrays[f"in_{name}_dram"] = a
        args.append(nc.dram_tensor(f"in_{name}_dram", a.shape, _mybir.dt.from_np(a.dtype), kind="ExternalInput").ap())
    for i, (shape, dtype) in enumerate(_OUTS):
        dt = _mybir.dt.from_np(_np.dtype(dtype))
        args.append(nc.dram_tensor(f"out_{i}_dram", shape, dt, kind="ExternalOutput").ap())
    cond_attention(nc, *args)
    r = _run(nc, [arrays], core_ids=[0])
    got = tuple(r.results[0][f"out_{i}_dram"] for i in range(len(_OUTS)))
    return got[0]
```

```python
from contextlib import ExitStack

import concourse.bass as bass
from concourse import mybir

F32 = mybir.dt.float32
BF16 = mybir.dt.bfloat16
ALU = mybir.AluOpType
ACT = mybir.ActivationFunctionType
AX = mybir.AxisListType

P = 128
NH = 16
Q, K, V, W, U = range(5)
Q_PIECES = (0, 0, 0, 1, 2, 1)
K_PIECES = (2, 1, 0, 0, 0, 1)


def cond_attention(nc: bass.Bass, x, cond, wq, wk, wv, ww, wu, out):
    B, S, H = x.shape
    D = H // NH
    HH = H // P
    TB = S // P
    NT = B * TB
    G = B * HH
    HG = NH // HH
    PG = HG // 2
    PAIRS = G * PG
    HEADS = 2 * PAIRS
    C = S // 512
    KR = len(Q_PIECES) * D
    ROWS = KR + 3
    VW = 2 * D
    STEPS = TB
    CH = TB * C
    TURN_BEFORE = 7
    EARLY = 3
    RUN = 16 * 3
    SCALE = float(D) ** -0.5

    x_v = x.rearrange("b (t p) h -> p (b t) h", p=P)
    out_v = out.rearrange("b (t p) h -> p (b t) h", p=P)
    w_in = (wq, wk, wv, ww, wu)
    piece_dram = [nc.dram_tensor(n, (G, KR // D, HG * D, S), BF16, kind="Internal").ap()
                  for n in ("q_pieces", "k_pieces")]
    den_dram = nc.dram_tensor("denominators", (HEADS, S), F32, kind="Internal").ap()
    rec_dram = nc.dram_tensor("reciprocals", (HEADS, S), F32, kind="Internal").ap()

    with ExitStack() as ctx:
        def sb(name, shape, dt):
            return ctx.enter_context(nc.sbuf_tensor(name, shape, dt))

        def sem(name):
            return ctx.enter_context(nc.semaphore(name))

        ps = ctx.enter_context(nc.psum_tensor("ps", [P, 8, 512], F32))
        MAX_BANKS, ST_BANK, PV_BANK = 3, 3, 7
        SPARE_BANK = 2
        JOB_BANKS = 5
        SUM_BANKS, IDLE_BANK = (0, 0, 2), 1

        X = sb("X", [P, NT, H], F32)
        xs = sb("xs", [P, NT, H], F32)
        xT = sb("xT", [P, HH, B * S], F32)
        Vall = sb("Vall", [P, G, TB, P], F32)
        prob = sb("prob", [P, 4, 2, S], F32)
        qst = sb("qst", [P, 4, 2, S], BF16)
        kst = sb("kst", [P, 4, 2, S], BF16)
        vbuf = sb("vbuf", [P, PG, TB, 2, VW], F32)
        ob = sb("ob", [P, 2, 512], F32)
        Wr = sb("Wr", [P, 5, HH, H], F32)
        Wsc = sb("Wsc", [P, 2, HH, H], F32)
        WT = sb("WT", [P, 3, HH, H], F32)
        WUT = sb("WUT", [P, 2, B, HH, H], F32)
        Mb = sb("Mb", [P, B, HH, H], F32)
        shared = sb("shared", [P, 7 * S], F32)
        AT = shared[:, 0:G * S].rearrange("p (g t) -> p g t", g=G)
        RD = shared[:, G * S:(G + 3) * S].rearrange("p (g t) -> p g t", g=3)
        full = shared[:, 0:2 * S].rearrange("p (i t) -> p i t", i=2)
        rest = shared[:, 2 * S:4 * S].rearrange("p (i t) -> p i t", i=2)
        pieces = shared[:, 4 * S:7 * S].bitcast(BF16).rearrange("p (i c t) -> p i c t", i=2, c=3)
        early = prob[:].rearrange("p s h t -> p (s h t)")
        wsty = early[:, 0:4 * HH * H].rearrange("p (i a h) -> p i a h", i=4, a=HH)
        WTsq = early[:, 4 * HH * H:7 * HH * H].rearrange("p (w a h) -> p w a h", w=3, a=HH)
        cb = sb("cb", [P, B, 2, H], F32)
        s2col = sb("s2col", [P, B, HH], F32)
        s1col = sb("s1col", [P, HH, B], F32)
        s1sq = sb("s1sq", [P, HH, B], F32)
        dsum = sb("dsum", [P, 5, B, HH], F32)
        dcoef = sb("dcoef", [P, 5, B, HH], F32)
        vs2 = sb("vs2", [P, B, HH], F32)
        stats = sb("stats", [P, NT, 6], F32)
        mv = sb("mv", [P, NT, 2], F32)
        vareps = sb("vareps", [P, NT], F32)
        rstd = sb("rstd", [P, NT], F32)
        minus_half = sb("minus_half", [P, 5 * G], F32)
        identf = sb("identf", [P, P], F32)
        identb = sb("identb", [P, P], BF16)
        mx = sb("mx", [P, 2, TB, C], F32)
        nm = sb("nm", [P, 2, TB], F32)
        nmr = sb("nmr", [P, 2, 2, TB], F32)
        mpc = sb("mpc", [P, 2, 3, TB], BF16)
        mT = sb("mT", [3 * TB, 4, P], BF16)
        denf = xs[:, 4, 0:S * (HEADS - 4) // P]
        denl = xs[:, 5, 0:S * 2 // P]
        rlast = xs[:, 6:8].rearrange("p a h -> p (a h)")
        yb = xs[:, 0:4]

        warm = sb("warm", [P, 1], F32)
        zeros = sb("zeros", [P, TB], F32)

        x_loaded = [sem(f"x_loaded{i}") for i in range(2 * B)]
        w_loaded = [sem(f"w_loaded{w}") for w in range(5)]
        cond_loaded = [sem(f"cond_loaded{b}") for b in range(B)]
        s1_loaded, s2_loaded = sem("s1_loaded"), sem("s2_loaded")
        s1_squared, sums_done, sums_ready = sem("s1_squared"), sem("sums_done"), sem("sums_ready")
        ident_ready, pool_own = sem("ident_ready"), sem("pool_own")
        styled, squared = sem("styled"), sem("squared")
        dcoef_ready, vs2_ready = sem("dcoef_ready"), sem("vs2_ready")
        dve_own, var_ready, rstd_ready, xhat_ready = sem("dve_own"), sem("var_ready"), sem("rstd_ready"), sem("xhat_ready")
        w_scaled = sem("w_scaled")
        job_done, job_emptied = sem("job_done"), sem("job_emptied")
        split_rest, split_last = sem("split_rest"), sem("split_last")
        first_stored = [sem(f"first_stored{i}") for i in range(2)]
        stored = [sem(f"stored{i}") for i in range(2)]
        stack_loaded = [sem(f"stack_loaded{i}") for i in range(4)]
        chunk_done, max_done, negmax_ready = sem("chunk_done"), sem("max_done"), sem("negmax_ready")
        negmax_split, msplit_own = sem("negmax_split"), sem("msplit_own")
        turned, mrow_copied = sem("turned"), sem("mrow_copied")
        mrow_loaded = [sem(f"mrow_loaded{i}") for i in range(4)]
        st_done, exp_done, pv_done = sem("st_done"), sem("exp_done"), sem("pv_done")
        v_ready, pv_free = sem("v_ready"), sem("pv_free")
        ob_moved = [sem(f"ob_moved{i}") for i in range(2)]
        k_ones_ready, v_ones_ready = sem("k_ones_ready"), sem("v_ones_ready")
        den_loaded, rec_ready, rec_stored, rd_loaded, at_ready = (
            sem("den_loaded"), sem("rec_ready"), sem("rec_stored"), sem("rd_loaded"), sem("at_ready"))
        rd_last, split_second, dcoef_own = sem("rd_last"), sem("split_second"), sem("dcoef_own")
        y_done, y_added = sem("y_done"), sem("y_added")
        y_stored = [sem(f"y_stored{i}") for i in range(4)]

        jobs = [("wt", w) for w in (Q, K, V)]
        jobs += [("xt", t) for t in range(TB // 2)]
        jobs += [("qk", 0, m, c) for m in (Q, K) for c in range(C)]
        jobs += [("v", t) for t in range(TB // 2)]
        jobs += [("xt", t) for t in range(TB // 2, TB)]
        jobs += [("v", TB // 2)] + [("qk", 1, m, c) for m in (Q, K) for c in range(C)]
        jobs += [("wu", 0, 0), ("v", TB // 2 + 1), ("wu", 1, 0), ("qk", 2, Q, 0), ("wu", 0, 1), ("qk", 2, Q, 1)]
        jobs += [("v", TB // 2 + 2), ("qk", 2, K, 0), ("wu", 1, 1), ("qk", 2, K, 1), ("m", 0)]
        jobs += [("qk", 3, Q, 0), ("qk", 3, Q, 1), ("v", TB - 1), ("qk", 3, K, 0), ("qk", 3, K, 1), ("m", 1)]
        FIRST_CHUNK = jobs.index(("qk", 1, Q, 0))
        AFTER = {"qk": 3, "v": 3, "m": 3, "wu": 1}
        REST_LAG, SECOND_LAG, THIRD_LAG = 2, 3, 3

        def chunks_after(n):
            if not FIRST_CHUNK <= n < len(jobs):
                return []
            total = EARLY * CH + 4
            at, upto = (min(total, sum(AFTER.get(j[0], 0) for j in jobs[FIRST_CHUNK:k])) for k in (n, n + 1))
            return [divmod(i, CH) for i in range(at, total if n == len(jobs) - 1 else upto)]

        def product_of(n):
            if 0 <= n < len(jobs) and jobs[n][0] == "qk" and jobs[n][1] and jobs[n][3] == C - 1:
                return qk_index(jobs[n][1], jobs[n][2])
            return None

        IDLE_PRODUCTS = {0: 20, 1: 14, 2: 34, 3: 10, 7: 6}

        def job_bank(n):
            return PV_BANK - (len(jobs) - 1 - n) % JOB_BANKS

        def score_bank(s, hd, last):
            return (ST_BANK, ST_BANK + 2, 0)[(2 * s + hd) % 3] if last else ST_BANK + 2 * hd

        def emptied(eng, n):
            eng.wait_ge(job_emptied, n + 1)

        def qk_index(g, m):
            return 2 * g + m

        LAST_BANKS = (3, 4, 5, 6, 7, 0, 1, 2)

        block = ctx.enter_context(nc.Block())

        @block.sync
        def _(sp):
            halves = range(0, TB, TB // 2)
            sp.dma_start(cb[:, 0], cond[0].rearrange("(s h) -> s h", s=2).partition_broadcast(P)).then_inc(cond_loaded[0], 16)
            for k, t in enumerate(halves):
                sp.dma_start(X[:, t:t + TB // 2], x_v[:, t:t + TB // 2]).then_inc(x_loaded[k], 16)
            sp.dma_start(cb[:, 1], cond[1].rearrange("(s h) -> s h", s=2).partition_broadcast(P)).then_inc(cond_loaded[1], 16)
            sp.dma_start(Wr[:, V], w_in[V].rearrange("(a p) h -> p a h", p=P)).then_inc(w_loaded[V], 16)
            for k, t in enumerate(halves):
                sp.dma_start(X[:, TB + t:TB + t + TB // 2], x_v[:, TB + t:TB + t + TB // 2]).then_inc(x_loaded[2 + k], 16)
            for w in (W, U):
                sp.dma_start(Wr[:, w], w_in[w].rearrange("(a p) h -> p a h", p=P)).then_inc(w_loaded[w], 16)
            for b in range(B):
                with nc.allow_non_contiguous_dma(reason="one style for each partition"):
                    sp.dma_start(s2col[:, b], cond[b, H:2 * H].rearrange("(a p) -> p a", p=P)).then_inc(s2_loaded, 16)

            def store_pieces(g, m, rows, done):
                i = qk_index(g, m)
                for c in range(3):
                    if c == 0:
                        emptied(sp, jobs.index(("qk", g, m, C - 1)))
                    elif c == 1:
                        sp.wait_ge(split_second, i + 1)
                    else:
                        sp.wait_ge(split_last, i + 1)
                    runs = [r for r, k in enumerate((Q_PIECES, K_PIECES)[m]) if k == c]
                    step = runs[1] - runs[0] if len(runs) > 1 else 1
                    dst = piece_dram[m][g, runs[0]:runs[-1] + 1:step, rows].rearrange("r p t -> p r t")
                    src = pieces[rows, i % 2, c:c + 1]
                    sp.dma_start(dst, src.to_broadcast([src.shape[0], len(runs), S])).then_inc(done, 16)

            def load_stacks(g, j, which=(Q, K)):
                for m in which:
                    stack = (qst, kst)[m]
                    for hd in range(2):
                        row = (2 * j + hd) * D
                        sp.dma_start(stack[0:KR, j, hd], piece_dram[m][g, :, row:row + D]).then_inc(stack_loaded[j], 16)

            def move_mrow(h, hg):
                sp.wait_ge(mrow_copied, h + 1)
                sp.dma_start(qst[KR:ROWS, hg // 2, hg % 2].rearrange("c (a t) -> c a t", a=TB),
                             mT[:, hg % 4]).then_inc(mrow_loaded[hg // 2], 16)

            def move_output(g, j):
                sp.wait_ge(pv_free, g * PG + j + 2)
                for hd in range(2):
                    for c in range(C):
                        row = 32 * (2 * hd + c)
                        sp.dma_start(AT[(2 * j + hd) * D:(2 * j + hd + 1) * D, g, c * 512:(c + 1) * 512],
                                     ob[row:row + D, j % 2]).then_inc(ob_moved[j % 2], 16)
                sp.dma_start(den_dram[bass.ds(g * HG + 2 * j, 2)].rearrange("h (c t) -> (h c) t", c=C),
                             ob[D:P:32, j % 2]).then_inc(ob_moved[j % 2], 16)

            first, others = slice(0, 2 * D), slice(2 * D, P)
            for m in (Q, K):
                store_pieces(0, m, first, first_stored[m])
            for m in (Q, K):
                sp.wait_ge(first_stored[m], RUN)
                load_stacks(0, 0, (m,))
            for m in (Q, K):
                store_pieces(0, m, others, stored[m])
            for i in range(2):
                sp.wait_ge(stored[i], RUN)
            load_stacks(0, 1)
            load_stacks(0, 2)
            for g in range(1, G):
                for m in (Q, K):
                    if (g, m) == (2, K):
                        move_mrow(0, 0)
                    if (g, m) == (3, Q):
                        move_mrow(1, 1)
                    store_pieces(g, m, slice(0, P), stored[m])
            for i in range(2):
                sp.wait_ge(stored[i], RUN * G)

            def rows(g, j):
                p = g * PG + j
                move_mrow(2 * p + 2, (2 * j + 2) % HG)
                move_mrow(2 * p + 3, (2 * j + 3) % HG)

            def pair(g, j):
                p = g * PG + j
                rows(g, j)
                sp.wait_ge(st_done, 2 * STEPS * (p + 1) + 1)
                load_stacks(g + (j + 3) // PG, (j + 3) % PG)
                move_output(g, j)

            with sp.Fori(0, G - 1) as g:
                for j in range(PG):
                    pair(g, j)

            def reciprocals(h0, n, tile, k):
                flat = den_dram[h0:h0 + n].rearrange("h t -> (h t)").rearrange("(p f) -> p f", p=P)
                back = rec_dram[h0:h0 + n].rearrange("h t -> (h t)").rearrange("(p f) -> p f", p=P)
                sp.dma_start(tile, flat).then_inc(den_loaded, 16)
                sp.wait_ge(rec_ready, k + 1)
                sp.dma_start(back, tile).then_inc(rec_stored, 16)
                sp.wait_ge(rec_stored, 16 * (k + 1))

            def spread(h, n, slot):
                sp.dma_start(RD[h % HG * D:(h % HG + n) * D, slot],
                             rec_dram[h:h + n].unsqueeze(1).to_broadcast([n, D, S])).then_inc(rd_loaded, 16)

            rows(G - 1, 0)
            sp.wait_ge(st_done, 2 * STEPS * ((G - 1) * PG + 1) + 1)
            load_stacks(G - 1, 3)
            move_output(G - 1, 0)
            rows(G - 1, 1)
            move_output(G - 1, 1)
            for i in range(2):
                sp.wait_ge(ob_moved[i], 16 * 5 * (2 * G - 1))
            rows(G - 1, 2)
            reciprocals(0, HEADS - 4, denf, 0)
            for g in range(G - 1):
                spread(g * HG, HG, g)
            move_output(G - 1, 2)
            sp.wait_ge(ob_moved[0], 16 * 5 * 2 * G)
            reciprocals(HEADS - 4, 2, denl, 1)
            sp.wait_ge(at_ready, 1)
            spread((G - 1) * HG, 6, 0)
            move_output(G - 1, 3)
            sp.wait_ge(rec_ready, 3)
            for hd in range(2):
                for c in range(C):
                    row = 32 * (2 * hd + c) + D
                    sp.dma_start(RD[(6 + hd) * D:(7 + hd) * D, 0, c * 512:(c + 1) * 512],
                                 rlast[row:row + D]).then_inc(rd_last, 16)

        @block.gpsimd
        def _(pool):
            nc.gpsimd.memset(identf[:], 0.0).then_inc(pool_own, 1)
            nc.gpsimd.memset(zeros[:], 0.0)
            nc.gpsimd.memset(minus_half[:], -0.5).then_inc(pool_own, 1)
            pool.wait_ge(pool_own, 2)
            nc.gpsimd.affine_select(out=identf[:], in_=identf[:], compare_op=ALU.not_equal, fill=1.0, base=0,
                                    pattern=[[-1, P]], channel_multiplier=1).then_inc(pool_own, 1)
            pool.wait_ge(pool_own, 3)
            nc.gpsimd.tensor_copy(identb[:], identf[:]).then_inc(ident_ready, 1)
            nc.gpsimd.memset(vbuf[:], 1.0).then_inc(v_ones_ready, 1)

            def inverse_roots(b):
                t = slice(b * TB // 2, (b + 1) * TB // 2)
                pool.wait_ge(var_ready, b + 1)
                nc.gpsimd.tensor_scalar(vareps[:, t], mv[:, t, 1], 1e-5, None, ALU.add).then_inc(pool_own, 1)
                pool.wait_ge(pool_own, 4 + b)
                nc.gpsimd.tensor_tensor(rstd[:, t], vareps[:, t], minus_half[:, 0:TB // 2], ALU.pow).then_inc(rstd_ready, 1)

            def demodulate(w0, n):
                sums, roots = (a[:, w0:w0 + n].rearrange("p w b a -> p (w b a)") for a in (dsum, dcoef))
                nc.gpsimd.tensor_tensor(roots, sums, minus_half[:, 0:G * n], ALU.pow).then_inc(dcoef_ready, 1)

            inverse_roots(0)
            inverse_roots(1)
            pool.wait_ge(sums_ready, 1)
            demodulate(Q, 2)
            inverse_roots(2)
            inverse_roots(3)
            pool.wait_ge(rstd_ready, 2 * B)
            nc.gpsimd.memset(kst[KR:ROWS, 2:4], 1.0).then_inc(k_ones_ready, 1)
            pool.wait_ge(k_ones_ready, 2)
            pool.wait_ge(squared, 2 * B * HH)
            sums = dsum[:, W:U + 1].rearrange("p w b a -> p (w b a)")
            nc.gpsimd.tensor_scalar(sums, sums, 1e-8, None, ALU.add).then_inc(dcoef_own, 1)
            pool.wait_ge(dcoef_own, 1)
            pool.wait_ge(sums_ready, 2)
            demodulate(V, 3)
            pool.wait_ge(dcoef_ready, 2)
            pool.wait_ge(s2_loaded, 32)
            nc.gpsimd.tensor_tensor(vs2[:].rearrange("p b a -> p (b a)"), dcoef[:, V].rearrange("p b a -> p (b a)"),
                                    s2col[:].rearrange("p b a -> p (b a)"), ALU.mult).then_inc(vs2_ready, 1)

            def split_max(h, hb):
                pool.wait_ge(negmax_ready, h + 1)
                nc.gpsimd.tensor_tensor(mpc[:, hb, 0], nm[:, hb], zeros[:], ALU.add).then_inc(msplit_own, 1)
                pool.wait_ge(msplit_own, 4 * h + 1)
                nc.gpsimd.tensor_tensor(nmr[:, hb, 0], nm[:, hb], mpc[:, hb, 0], ALU.subtract).then_inc(msplit_own, 1)
                pool.wait_ge(msplit_own, 4 * h + 2)
                nc.gpsimd.tensor_tensor(mpc[:, hb, 1], nmr[:, hb, 0], zeros[:], ALU.add).then_inc(msplit_own, 1)
                pool.wait_ge(msplit_own, 4 * h + 3)
                nc.gpsimd.tensor_tensor(nmr[:, hb, 1], nmr[:, hb, 0], mpc[:, hb, 1], ALU.subtract).then_inc(msplit_own, 1)
                pool.wait_ge(msplit_own, 4 * h + 4)
                nc.gpsimd.tensor_tensor(mpc[:, hb, 2], nmr[:, hb, 1], zeros[:], ALU.add).then_inc(negmax_split, 1)

            def values(g, j):
                nc.gpsimd.tensor_copy(vbuf[:, j, :, :, 0:D],
                                      Vall[:, g, :, 2 * j * D:2 * (j + 1) * D].rearrange("p t (h d) -> p t h d", h=2)
                                      ).then_inc(v_ready, 1)

            for n in range(len(jobs) + THIRD_LAG):
                job = jobs[n] if n < len(jobs) else ()
                if job == ("v", TB // 2 - 1):
                    emptied(pool, n)
                    pool.wait_ge(v_ones_ready, 1)
                    values(0, 0)
                i = product_of(n - THIRD_LAG)
                if i is not None:
                    pool.wait_ge(split_second, i + 1)
                    nc.gpsimd.tensor_tensor(pieces[:, i % 2, 2], rest[:, i % 2], pieces[:, i % 2, 1],
                                            ALU.subtract).then_inc(split_last, 1)
                for h, i in chunks_after(n):
                    if i == CH - 1:
                        split_max(h, h % 2)

            emptied(pool, jobs.index(("v", TB - 1)))

            with pool.Fori(0, G - 1) as g:
                for j in range(PG):
                    p = g * PG + j
                    split_max(2 * p + 3, 1)
                    values(g + (j + 1) // PG, (j + 1) % PG)
                    split_max(2 * p + 4, 0)
            for j in range(PG - 1):
                p = (G - 1) * PG + j
                values(G - 1, j + 1)
                split_max(2 * p + 3, 1)
                if 2 * p + 4 < HEADS:
                    split_max(2 * p + 4, 0)

        @block.vector
        def _(dve):
            own = [0]

            def after(ins):
                own[0] += 1
                ins.then_inc(dve_own, 1)
                dve.wait_ge(dve_own, own[0])

            def norm_stats(k):
                t = slice(k * TB // 2, (k + 1) * TB // 2)
                dve.wait_ge(x_loaded[k], 16)
                after(nc.vector.tensor_tensor(xs[:, t], X[:, t], cb[:, k // 2, 0:1].to_broadcast([P, TB // 2, H]), ALU.mult))
                for i in range(t.start, t.stop):
                    last = nc.vector.bn_stats(stats[:, i], xs[:, i])
                after(last)
                for i in range(t.start, t.stop):
                    last = nc.vector.bn_aggr(mv[:, i], stats[:, i])
                last.then_inc(var_ready, 1)

            def norm_apply(k):
                dve.wait_ge(rstd_ready, k + 1)
                for i in range(k * TB // 2, (k + 1) * TB // 2):
                    nc.vector.tensor_scalar(xs[:, i], xs[:, i], mv[:, i, 0:1], rstd[:, i:i + 1],
                                            ALU.subtract, ALU.mult).then_inc(xhat_ready, 1)

            def style(n, w, b):
                dve.wait_ge(w_loaded[w], 16)
                nc.vector.tensor_tensor(wsty[:, n], Wr[:, w], cb[:, b, 1:2].to_broadcast([P, HH, H]),
                                        ALU.mult).then_inc(styled, 1)

            nc.vector.memset(kst[KR:ROWS, 0:2], 1.0).then_inc(k_ones_ready, 1)
            dve.wait_ge(cond_loaded[0], 16)
            norm_stats(0)
            norm_stats(1)
            norm_apply(0)
            norm_apply(1)

            def take_sums(w0, n):
                dve.wait_ge(sums_done, w0 + n)
                nc.vector.tensor_scalar(dsum[:, w0:w0 + n].rearrange("p w b a -> p w a b"),
                                        ps[:, SUM_BANKS[w0], w0 * G:(w0 + n) * G].rearrange("p (w a b) -> p w a b", w=n, a=HH),
                                        1e-8, None, ALU.add).then_inc(sums_ready, 1)

            take_sums(Q, 2)
            dve.wait_ge(cond_loaded[1], 16)
            norm_stats(2)
            norm_stats(3)
            take_sums(V, 1)

            def reduce_chunk(h, i, hb):
                bank = (i if i < TURN_BEFORE else i + 1) % MAX_BANKS
                dve.wait_ge(chunk_done, h * CH + i + 1)
                nc.vector.tensor_reduce(mx[:, hb, i // C, i % C:i % C + 1], ps[:, bank], AX.X, ALU.max).then_inc(max_done, 1)
                if i == CH - 1:
                    dve.wait_ge(max_done, (h + 1) * CH)
                    nc.vector.tensor_reduce(nm[:, hb], mx[:, hb], AX.X, ALU.max, negate=True).then_inc(negmax_ready, 1)

            def split_rest_of(i, n):
                emptied(dve, n)
                if i >= 2:
                    dve.wait_ge(split_last, i - 1)
                nc.vector.tensor_tensor(rest[:, i % 2], full[:, i % 2], pieces[:, i % 2, 0],
                                        ALU.subtract).then_inc(split_rest, 1)

            for n in range(len(jobs) + REST_LAG):
                job = jobs[n] if n < len(jobs) else ("",)
                if job == ("v", 0):
                    norm_apply(2)
                    norm_apply(3)
                if job[0] == "xt" and 0 <= job[1] - TB // 2 < 2:
                    for b in range(B):
                        k = (job[1] - TB // 2) * B + b
                        style(k, W + k // B, b)
                if job[0] == "qk" and job[1] == 0 and job[3] == C - 1:
                    i = qk_index(0, job[2])
                    split_rest_of(i, n)
                    dve.wait_ge(split_rest, i + 1)
                    nc.vector.tensor_copy(pieces[:, i % 2, 1], rest[:, i % 2]).then_inc(split_second, 1)
                    dve.wait_ge(split_second, i + 1)
                    nc.vector.tensor_tensor(pieces[:, i % 2, 2], rest[:, i % 2], pieces[:, i % 2, 1],
                                            ALU.subtract).then_inc(split_last, 1)
                i = product_of(n - REST_LAG)
                if i is not None:
                    split_rest_of(i, n - REST_LAG)
                for h, i in chunks_after(n):
                    reduce_chunk(h, i, h % 2)
            for i in range(4, CH):
                reduce_chunk(EARLY, i, EARLY % 2)
            with dve.Fori(0, (HEADS - EARLY - 1) // 2) as r:
                for k in range(2):
                    for i in range(CH):
                        reduce_chunk(2 * r + (EARLY + 1 + k), i, k)

            def add(t, bank):
                dve.wait_ge(y_done, t + 1)
                if t >= 4:
                    dve.wait_ge(y_stored[t % 4], 16 * (t // 4))
                nc.vector.tensor_tensor(yb[:, t % 4], ps[:, bank, 0:H], X[:, t], ALU.add).then_inc(y_added, 1)

            dve.wait_ge(den_loaded, 16)
            nc.vector.reciprocal(denf, denf).then_inc(rec_ready, 1)
            for g in range(G - 1):
                dve.wait_ge(rd_loaded, 16 * (G - 1))
                nc.vector.tensor_tensor(AT[:, g], AT[:, g], RD[:, g], ALU.mult).then_inc(at_ready, 1)
            dve.wait_ge(den_loaded, 32)
            nc.vector.reciprocal(denl, denl).then_inc(rec_ready, 1)
            dve.wait_ge(pv_free, PAIRS + 1)
            nc.vector.reciprocal(rlast, ob[:, (PAIRS - 1) % 2]).then_inc(rec_ready, 1)
            for t in range(TB):
                add(t, t % 3)
            dve.wait_ge(rd_loaded, 16 * G)
            dve.wait_ge(rd_last, 64)
            for i in range(2):
                dve.wait_ge(ob_moved[i], 80 * 2 * G)
            nc.vector.tensor_tensor(AT[:, G - 1], AT[:, G - 1], RD[:, 0], ALU.mult).then_inc(at_ready, 1)
            for t in range(TB, NT):
                add(t, LAST_BANKS[t - TB])

        @block.scalar
        def _(act):
            act.dma_start(Wr[:, Q], w_in[Q].rearrange("(a p) h -> p a h", p=P)).then_inc(w_loaded[Q], 16)
            act.dma_start(Wr[:, K], w_in[K].rearrange("(a p) h -> p a h", p=P)).then_inc(w_loaded[K], 16)
            for b in range(B):
                with nc.allow_non_contiguous_dma(reason="one style for each partition"):
                    act.dma_start(s1col[:, :, b], cond[b, 0:H].rearrange("(a p) -> p a", p=P)).then_inc(s1_loaded, 16)
            act.wait_ge(ident_ready, 1)
            nc.scalar.activation(warm[:], identf[:, 0:1], ACT.Exp)

            def square_styles():
                act.wait_ge(s1_loaded, 16 * B)
                nc.scalar.activation(s1sq[:].rearrange("p a b -> p (a b)"), s1col[:].rearrange("p a b -> p (a b)"),
                                     ACT.Square).then_inc(s1_squared, 1)

            def squares(n, w, b):
                act.wait_ge(styled, n + 1)
                for a in range(HH):
                    nc.scalar.activation(wsty[:, n, a], wsty[:, n, a], ACT.Square,
                                         accum_out=dsum[:, w, b, a:a + 1]).then_inc(squared, 1)

            def copy_mrow(h, hq):
                act.wait_ge(turned, h + 1)
                nc.scalar.copy(mT[:, hq], ps[0:3 * TB, TURN_BEFORE % MAX_BANKS].bitcast(BF16)[:, 0:P]).then_inc(mrow_copied, 1)

            def exps(n, s, last=False):
                for hd in range(2):
                    bank = score_bank(s, hd, last)
                    act.wait_ge(st_done, 2 * n + hd + 1)
                    if not isinstance(n, int) or n >= 4:
                        act.wait_ge(pv_done, n - 3)
                    nc.scalar.activation(prob[:, s % 4, hd], ps[:, bank:bank + 2].rearrange("p c t -> p (c t)"),
                                         ACT.Exp, scale=SCALE).then_inc(exp_done, 1)

            def round_second(i):
                act.wait_ge(split_rest, i + 1)
                nc.scalar.copy(pieces[:, i % 2, 1], rest[:, i % 2]).then_inc(split_second, 1)

            for n in range(len(jobs)):
                if n == 2:
                    square_styles()
                if n == len(jobs) - 1:
                    act.wait_ge(squared, 2 * B * HH)
                    act.wait_ge(sums_done, 3)
                    exps(0, 0)
                i = product_of(n - SECOND_LAG)
                if i is not None:
                    round_second(i)
                job = jobs[n]
                for k in {16: (0,), 17: (1,), 18: (2,), 19: (3,)}.get(n, ()):
                    squares(k, W + k // B, k % B)
                bank = job_bank(n)
                act.wait_ge(job_done, n + 1)
                if job[0] == "wt":
                    nc.scalar.copy(WT[:, job[1]].rearrange("p a o -> p (a o)"), ps[:, bank])
                    nc.scalar.activation(WTsq[:, job[1]].rearrange("p a o -> p (a o)"), ps[:, bank],
                                         ACT.Square).then_inc(job_emptied, 1)
                if job[0] == "xt":
                    nc.scalar.copy(xT[:, :, job[1] * 2 * P:(job[1] + 1) * 2 * P],
                                   ps[:, bank].rearrange("p (a t) -> p a t", a=HH)).then_inc(job_emptied, 1)
                if job[0] == "qk":
                    _, g, m, c = job
                    i = qk_index(g, m)
                    act.wait_ge(dcoef_ready, 1)
                    if i >= 2:
                        act.wait_ge(split_rest, i - 1)
                        act.wait_ge(stored[m], RUN * g)
                    col = slice(c * 512, (c + 1) * 512)
                    scale = dcoef[:, m, g // HH, g % HH:g % HH + 1]
                    nc.scalar.activation(full[:, i % 2, col], ps[:, bank], ACT.Copy, scale=scale)
                    nc.scalar.activation(pieces[:, i % 2, 0, col], ps[:, bank], ACT.Copy, scale=scale).then_inc(job_emptied, 1)
                if job[0] == "v":
                    t = job[1] * 2
                    b = t // TB
                    nc.scalar.copy(Vall[:, b * HH:(b + 1) * HH, t % TB:t % TB + 2],
                                   ps[:, bank].rearrange("p (t a o) -> p a t o", t=2, a=HH)).then_inc(job_emptied, 1)
                if job[0] == "wu":
                    _, i, b = job
                    act.wait_ge(vs2_ready, 1)
                    for a in range(HH):
                        last = nc.scalar.activation(WUT[:, i, b, a], ps[:, bank, a * H:(a + 1) * H], ACT.Copy,
                                                    scale=vs2[:, b, a:a + 1])
                    last.then_inc(job_emptied, 1)
                if job[0] == "m":
                    nc.scalar.copy(Mb[:, job[1]].rearrange("p a o -> p (a o)"),
                                   ps[:, bank]).then_inc(pv_free if n == len(jobs) - 1 else job_emptied, 1)
                ahead = jobs[n + 2] if n + 2 < len(jobs) else ("",)
                if ahead[0] == "wu":
                    _, i, b = ahead
                    act.wait_ge(dcoef_ready, 2)
                    for a in range(HH):
                        last = nc.scalar.activation(Wsc[:, i, a], Wr[:, W + i, a], ACT.Copy,
                                                    scale=dcoef[:, W + i, b, a:a + 1])
                    last.then_inc(w_scaled, 1)
                for h, i in chunks_after(n):
                    if i == TURN_BEFORE and h:
                        copy_mrow(h - 1, (h - 1) % 4)

            def pair(i, half, p, last_m):
                for s in range(1, STEPS):
                    exps(p * STEPS + s, s, last=last_m is not None and p == PAIRS - 1)
                    if last_m is not None and p == 0 and s == 1:
                        round_second(2 * G - 1)
                    if s == 1 and (last_m is None or 2 * p + 2 <= last_m):
                        copy_mrow(2 * p + 2, (2 * half + 2) % 4)
                    if s == 5 and (last_m is None or 2 * p + 3 <= last_m):
                        copy_mrow(2 * p + 3, (2 * half + 3) % 4)
                if last_m is None or p < PAIRS - 1:
                    exps((p + 1) * STEPS, 0)
                act.wait_ge(pv_done, (p + 1) * STEPS)
                if last_m is None or p >= 2:
                    act.wait_ge(ob_moved[half], 80 * i)
                nc.scalar.copy(ob[:, half], ps[:, PV_BANK]).then_inc(pv_free, 1)

            for p in range(2):
                pair(0, p, p, HEADS - 1)
            with act.Fori(1, PAIRS // 2 - 1) as i:
                for half in range(2):
                    pair(i, half, 2 * i + half, None)
            for p in (PAIRS - 2, PAIRS - 1):
                pair(p // 2, p % 2, p, HEADS - 1)
            for t in range(NT):
                act.wait_ge(y_added, t + 1)
                act.dma_start(out_v[:, t], yb[:, t % 4]).then_inc(y_stored[t % 4], 16)
            for i in range(4):
                act.wait_ge(y_stored[i], 16 * NT // 4)

        @block.tensor
        def _(pe):
            def form_chunk(h, i, slot, hd, first):
                bank = (i if i < TURN_BEFORE else i + 1) % MAX_BANKS
                if i == TURN_BEFORE + 2:
                    if not (isinstance(h, int) and h == 0):
                        pe.wait_ge(mrow_copied, h)
                    else:
                        pe.wait_ge(max_done, TURN_BEFORE - 2)
                else:
                    need = {0: -1, 1: 0, 2: -2, TURN_BEFORE: i - 1, TURN_BEFORE + 1: i - 1}.get(i, i - 2)
                    if not first or i >= 3:
                        pe.wait_ge(max_done, h * CH + need)
                qt, kc = divmod(i, C)
                nc.tensor.matmul(ps[:, bank], qst[0:KR, slot, hd, qt * P:(qt + 1) * P],
                                 kst[0:KR, slot, hd, kc * 512:(kc + 1) * 512], start=True, stop=True).then_inc(chunk_done, 1)

            def turn_max(h, hb, own_chunks):
                pe.wait_ge(negmax_split, h + 1)
                pe.wait_ge(max_done, own_chunks)
                nc.tensor.transpose(ps[0:3 * TB, TURN_BEFORE % MAX_BANKS].bitcast(BF16)[:, 0:P],
                                    mpc[:, hb].rearrange("p c t -> p (c t)"), identb[:]).then_inc(turned, 1)

            def chunk(h, i, slot, hd, first=False):
                if i == TURN_BEFORE and not first:
                    turn_max(h - 1, 1 - hd, h * CH + TURN_BEFORE - 2)
                form_chunk(h, i, slot, hd, first)

            def stack_ready(g, j):
                pe.wait_ge(stack_loaded[j], 64 * (g + 1))

            def half_scores(n, s, slot, hd, last=False):
                if last and s >= 1:
                    pe.wait_ge(exp_done, 2 * n + hd - 2)
                elif not isinstance(n, int) or n >= 1:
                    pe.wait_ge(exp_done, 2 * n + hd - 1)
                bank = score_bank(s, hd, last)
                for c in range(C):
                    done = nc.tensor.matmul(ps[:, bank + c], kst[0:ROWS, slot, hd, s * P:(s + 1) * P],
                                            qst[0:ROWS, slot, hd, c * 512:(c + 1) * 512], start=True, stop=True)
                done.then_inc(st_done, 1)

            def sums_of_squares(w):
                emptied(pe, jobs.index(("wt", w)))
                for o in range(HH):
                    for a in range(HH):
                        last = nc.tensor.matmul(ps[:, SUM_BANKS[w], (w * HH + o) * B:(w * HH + o + 1) * B],
                                                WTsq[:, w, a, o * P:(o + 1) * P], s1sq[:, a],
                                                start=(a == 0), stop=(a == HH - 1))
                last.then_inc(sums_done, 1)

            between = []

            def next_chunks(count):
                for _ in range(min(count, len(between))):
                    h, i = between.pop(0)
                    if (h, i) == (0, 0):
                        pe.wait_ge(sums_ready, 2)
                    if i == 0 and h % 2 == 0:
                        stack_ready(0, h // 2)
                    chunk(h, i, h // 2, h % 2, first=(h == 0))

            pe.wait_ge(ident_ready, 1)
            for n, job in enumerate(jobs):
                between += chunks_after(n)
                for _ in range(IDLE_PRODUCTS.get(n, 0)):
                    nc.tensor.matmul(ps[:, IDLE_BANK, 0:P], identb[:], identb[:], start=True, stop=True)
                if n == 2:
                    pe.wait_ge(s1_squared, 1)
                    sums_of_squares(Q)
                    sums_of_squares(K)
                if n == 7:
                    sums_of_squares(V)
                bank = job_bank(n)
                if n == len(jobs) - 1:
                    pe.wait_ge(k_ones_ready, 2)
                    pe.wait_ge(mrow_loaded[0], 32)
                    for hd in range(2):
                        emptied(pe, n - JOB_BANKS + 2 * (hd + 1))
                        half_scores(0, 0, 0, hd)
                if n >= JOB_BANKS:
                    emptied(pe, n - JOB_BANKS)
                if job[0] == "wt":
                    w = job[1]
                    pe.wait_ge(w_loaded[w], 16)
                    for a in range(HH):
                        for o in range(HH):
                            last = nc.tensor.transpose(ps[:, bank, a * H + o * P:a * H + (o + 1) * P],
                                                       Wr[:, w, o, a * P:(a + 1) * P], identf[:])
                if job[0] == "xt":
                    t = 2 * job[1]
                    pe.wait_ge(xhat_ready, t + 2)
                    for a in range(HH):
                        for o in range(2):
                            last = nc.tensor.transpose(ps[:, bank, a * H + o * P:a * H + (o + 1) * P],
                                                       xs[:, t + o, a * P:(a + 1) * P], identf[:])
                if job[0] == "qk":
                    _, g, m, c = job
                    b, half = divmod(g, HH)
                    if (m, c) == (Q, 0):
                        emptied(pe, jobs.index(("xt", (b + 1) * TB // 2 - 1)))
                    for a in range(HH):
                        last = nc.tensor.matmul(ps[:, bank], WT[:, m, a, half * P:(half + 1) * P],
                                                xT[:, a, b * S + c * 512:b * S + (c + 1) * 512],
                                                start=(a == 0), stop=(a == HH - 1))
                        if a == 0:
                            next_chunks(1)
                if job[0] == "v":
                    t = 2 * job[1]
                    emptied(pe, jobs.index(("xt", job[1])))
                    for o in range(2):
                        for a in range(HH):
                            last = nc.tensor.matmul(ps[:, bank, o * H:(o + 1) * H], xT[:, a, (t + o) * P:(t + o + 1) * P],
                                                    WT[:, V, a], start=(a == 0), stop=(a == HH - 1))
                        if o == 0:
                            next_chunks(1)
                if job[0] == "wu":
                    _, i, b = job
                    pe.wait_ge(w_scaled, 2 * b + i + 1)
                    for a in range(HH):
                        for o in range(HH):
                            last = nc.tensor.transpose(ps[:, bank, a * H + o * P:a * H + (o + 1) * P],
                                                       Wsc[:, i, o, a * P:(a + 1) * P], identf[:])
                if job[0] == "m":
                    b = job[1]
                    emptied(pe, jobs.index(("wu", 1, b)))
                    for o in range(HH):
                        for a in range(HH):
                            last = nc.tensor.matmul(ps[:, bank, o * H:(o + 1) * H], Wr[:, V, a, o * P:(o + 1) * P],
                                                    WUT[:, 1, b, a], start=(a == 0), stop=(a == HH - 1))
                        if o == 0:
                            next_chunks(1)
                last.then_inc(job_done, 1)
                next_chunks(len(between))

            def weigh_values(n, s, j):
                pe.wait_ge(exp_done, 2 * n + 2)
                for hd in range(2):
                    for c in range(C):
                        row = 32 * (2 * hd + c)
                        last = nc.tensor.matmul(ps[row:row + VW, PV_BANK], vbuf[:, j, s, hd],
                                                prob[:, s % 4, hd, c * 512:(c + 1) * 512],
                                                start=(s == 0), stop=(s == STEPS - 1), tile_position=(0, row))
                last.then_inc(pv_done, 1)

            def step(g, j, s, final):
                p = g * PG + j
                n = p * STEPS + s
                k = 2 * j + 3 + s // 4
                head_chunks = [(g * HG + k, (k % HG) // 2, k % 2, 4 * (s % 4) + i) for i in range(4)]
                if final and k >= HG:
                    head_chunks = []
                if s == 0:
                    pe.wait_ge(mrow_loaded[j], 32 * (g + 1))
                if s == 4 and head_chunks:
                    stack_ready(g + k // HG, (k % HG) // 2)
                half_scores(n, s, j, 0, last=final and j == PG - 1)
                for h, slot, hd, i in head_chunks[:1]:
                    chunk(h, i, slot, hd)
                half_scores(n, s, j, 1, last=final and j == PG - 1)
                for h, slot, hd, i in head_chunks[1:3]:
                    chunk(h, i, slot, hd)
                if s == 1:
                    pe.wait_ge(v_ready, p + 1)
                    pe.wait_ge(pv_free, p + 1)
                if s >= 1:
                    weigh_values(n - 1, s - 1, j)
                elif not (isinstance(p, int) and p == 0):
                    weigh_values(n - 1, STEPS - 1, (j - 1) % PG)
                if final and k == HG and s == 5:
                    turn_max(HEADS - 1, 1, HEADS * CH)
                for h, slot, hd, i in head_chunks[3:]:
                    chunk(h, i, slot, hd)

            def part(t, bank, chunks):
                b = t // TB
                for a in chunks:
                    if a < HH:
                        left, right = xT[:, a, t * P:(t + 1) * P], Mb[:, b, a]
                    else:
                        left, right = AT[:, b * HH + a - HH, (t % TB) * P:(t % TB + 1) * P], WUT[:, 0, b, a - HH]
                    last = nc.tensor.matmul(ps[:, bank, 0:H], left, right, start=(a == 0), stop=(a == 2 * HH - 1))
                return last

            def group(g, final):
                for j in range(PG):
                    for s in range(1, STEPS):
                        step(g, j, s, final)
                    if j < PG - 1:
                        step(g, j + 1, 0, final)
                    elif not final:
                        step(g + 1, 0, 0, False)
                    else:
                        part(SPARE_BANK, SPARE_BANK, range(HH))
                        weigh_values(PAIRS * STEPS - 1, STEPS - 1, PG - 1)

            with pe.Fori(0, G - 1) as g:
                group(g, False)
            group(G - 1, True)

            pe.wait_ge(at_ready, G - 1)
            for t in range(TB):
                if t >= 3:
                    pe.wait_ge(y_added, t - 2)
                part(t, t % 3, range(HH if t == SPARE_BANK else 0, 2 * HH)).then_inc(y_done, 1)
            pe.wait_ge(pv_free, PAIRS + 1)
            for i in range(4):
                part(TB + i, LAST_BANKS[i], range(2 * HH - 1))
            pe.wait_ge(at_ready, G)
            for i, bank in enumerate(LAST_BANKS):
                if bank < MAX_BANKS:
                    pe.wait_ge(y_added, TB)
                part(TB + i, bank, range(2 * HH - 1 if i < 4 else 0, 2 * HH)).then_inc(y_done, 1)


_INS = ["x", "cond_2048", "L0_cond_q_weight", "L0_cond_k_weight", "L0_cond_v_weight", "L0_cond_w_weight",
        "L0_cond_u_weight"]
_OUTS = [((2, 1024, 256), "float32")]


def kernel(**inputs):
    import numpy as _np
    import concourse.bacc as _bacc
    from concourse import mybir as _mybir
    from concourse.bass_utils import run_bass_kernel_spmd as _run

    nc = _bacc.Bacc("TRN2", target_bir_lowering=False, num_devices=1)
    arrays, args = {}, []
    for name in _INS:
        a = _np.ascontiguousarray(inputs[name])
        arrays[f"in_{name}_dram"] = a
        args.append(nc.dram_tensor(f"in_{name}_dram", a.shape, _mybir.dt.from_np(a.dtype), kind="ExternalInput").ap())
    for i, (shape, dtype) in enumerate(_OUTS):
        dt = _mybir.dt.from_np(_np.dtype(dtype))
        args.append(nc.dram_tensor(f"out_{i}_dram", shape, dt, kind="ExternalOutput").ap())
    cond_attention(nc, *args)
    r = _run(nc, [arrays], core_ids=[0])
    got = tuple(r.results[0][f"out_{i}_dram"] for i in range(len(_OUTS)))
    return got[0]
```
